# Optimizing a Trainium2 kernel written in Bass

```python
import numpy as np
import jax
import jax.numpy as jnp

def _softmax(x, axis=-1):
    return jax.nn.softmax(x, axis=axis)

def _gelu(x):
    return jax.nn.gelu(x, approximate=True)

def _silu(x):
    return jax.nn.silu(x)

def _sigmoid(x):
    return jax.nn.sigmoid(x)

def _layernorm(x, axis=-1, eps=1e-05):
    m = jnp.mean(x, axis=axis, keepdims=True)
    v = jnp.var(x, axis=axis, keepdims=True)
    return (x - m) / jnp.sqrt(v + eps)

def _scatter_add(tgt, idx, src, axis=0):
    return tgt.at[idx].add(src)

def _segment_sum(src, seg, n):
    return jax.ops.segment_sum(src, seg, n)
kernel_name = 'mk_seq_preln_d1_jaxref_r8_4b14d4'

def setup_inputs(seed: int=0):
    np.random.seed(seed)
    _w = jnp.asarray

    def _L0_attn_setup():
        import jax, jax.numpy as jnp
        import numpy as np
        HEADS = 16

        def _fm(t):
            return jax.nn.elu(t) + 1.0
        key = jax.random.key(seed)
        ks = jax.random.split(key, 9)
        B, N, D = (4, 1024, 128)
        s = 1.0 / np.sqrt(D)
        return {'x': jax.random.normal(ks[0], (B, N, D), dtype=jnp.float32), 'wq': jax.random.normal(ks[1], (D, D), dtype=jnp.float32) * s, 'bq': jnp.zeros((D,), dtype=jnp.float32), 'wk': jax.random.normal(ks[2], (D, D), dtype=jnp.float32) * s, 'bk': jnp.zeros((D,), dtype=jnp.float32), 'wv': jax.random.normal(ks[3], (D, D), dtype=jnp.float32) * s, 'bv': jnp.zeros((D,), dtype=jnp.float32), 'wo': jax.random.normal(ks[4], (D, D), dtype=jnp.float32) * s, 'bo': jnp.zeros((D,), dtype=jnp.float32)}
    _L0_attn_in = _L0_attn_setup()

    def _L0_ffn_setup():
        import jax, jax.numpy as jnp
        import numpy as np
        B, S, D, E, F = (2, 256, 128, 8, 512)
        key = jax.random.key(seed)
        ks = jax.random.split(key, 4)
        return {'hidden_states': jax.random.normal(ks[0], (B, S, D), dtype=jnp.float32), 'Wr': jax.random.normal(ks[1], (D, E), dtype=jnp.float32) * (1.0 / np.sqrt(D)), 'W1': jax.random.normal(ks[2], (E, D, F), dtype=jnp.float32) * (1.0 / np.sqrt(D)), 'b1': jnp.zeros((E, F), dtype=jnp.float32), 'W2': jax.random.normal(ks[3], (E, F, D), dtype=jnp.float32) * (1.0 / np.sqrt(F)), 'b2': jnp.zeros((E, D), dtype=jnp.float32)}
    _L0_ffn_in = _L0_ffn_setup()
    _d = {'L0_attn_x': _L0_attn_in['x'], 'L0_attn_wq': _L0_attn_in['wq'], 'L0_attn_bq': _L0_attn_in['bq'], 'L0_attn_wk': _L0_attn_in['wk'], 'L0_attn_bk': _L0_attn_in['bk'], 'L0_attn_wv': _L0_attn_in['wv'], 'L0_attn_bv': _L0_attn_in['bv'], 'L0_attn_wo': _L0_attn_in['wo'], 'L0_attn_bo': _L0_attn_in['bo'], 'L0_ffn_Wr': _L0_ffn_in['Wr'], 'L0_ffn_W1': _L0_ffn_in['W1'], 'L0_ffn_b1': _L0_ffn_in['b1'], 'L0_ffn_W2': _L0_ffn_in['W2'], 'L0_ffn_b2': _L0_ffn_in['b2']}
    _x0 = _d['L0_attn_x']
    _d['L0_attn_x'] = jax.random.normal(jax.random.fold_in(jax.random.key(seed), 1), (4, 512, 128), dtype=_x0.dtype)
    del _x0
    return _d

def reference(L0_attn_x, L0_attn_wq, L0_attn_bq, L0_attn_wk, L0_attn_bk, L0_attn_wv, L0_attn_bv, L0_attn_wo, L0_attn_bo, L0_ffn_Wr, L0_ffn_W1, L0_ffn_b1, L0_ffn_W2, L0_ffn_b2):

    def _L0_attn_ref(x, wq, bq, wk, bk, wv, bv, wo, bo):
        import jax, jax.numpy as jnp
        import numpy as np
        HEADS = 16

        def _fm(t):
            return jax.nn.elu(t) + 1.0
        B, N, D = x.shape
        H = HEADS
        Dh = D // H
        q = _fm((x @ wq + bq).reshape(B, N, H, Dh))
        k = _fm((x @ wk + bk).reshape(B, N, H, Dh))
        v = (x @ wv + bv).reshape(B, N, H, Dh)
        kv = jnp.einsum('bnhd,bnhe->bhde', k, v)
        z = 1.0 / (jnp.einsum('bnhd,bhd->bnh', q, k.sum(axis=1)) + 1e-06)
        scores = jnp.einsum('bnhd,bhde,bnh->bnhe', q, kv, z)
        out = scores.reshape(B, N, D) @ wo + bo
        return out

    def _L0_ffn_ref(hidden_states, Wr, W1, b1, W2, b2):
        import jax, jax.numpy as jnp
        import numpy as np
        B, S, D, E, F = (2, 256, 128, 8, 512)
        b, s, d = hidden_states.shape
        e = Wr.shape[1]
        x = hidden_states.reshape(b * s, d)
        router_logits = x @ Wr
        router_probs = jax.nn.softmax(router_logits, axis=-1)
        expert_idx = jnp.argmax(router_probs, axis=-1)
        p_max = jnp.max(router_probs, axis=-1, keepdims=True)

        def expert_mlp(w1, bb1, w2, bb2):
            h = jax.nn.gelu(x @ w1 + bb1, approximate=False)
            return h @ w2 + bb2
        outs = jax.vmap(expert_mlp)(W1, b1, W2, b2)
        onehot = jax.nn.one_hot(expert_idx, e, dtype=x.dtype)
        next_states = jnp.einsum('te,etd->td', onehot, outs)
        out = p_max * next_states
        return out.reshape(b, s, d)
    x = L0_attn_x
    x = x + _L0_attn_ref(_layernorm(x, axis=-1), L0_attn_wq, L0_attn_bq, L0_attn_wk, L0_attn_bk, L0_attn_wv, L0_attn_bv, L0_attn_wo, L0_attn_bo)
    x = x + _L0_ffn_ref(_layernorm(x, axis=-1), L0_ffn_Wr, L0_ffn_W1, L0_ffn_b1, L0_ffn_W2, L0_ffn_b2)
    return x

_drawn_inputs = setup_inputs


def setup_inputs(seed=0):
    import zlib

    import numpy as np

    out = dict(_drawn_inputs(seed))
    spreads = {'L0_attn_bq': (0.0, 2.0),
     'L0_attn_bk': (0.0, 2.0),
     'L0_attn_bv': (0.0, 0.1),
     'L0_attn_bo': (0.0, 0.1),
     'L0_ffn_b1': (0.0, 0.314),
     'L0_ffn_b2': (0.0, 0.1)}
    factors = {}
    for name, (base, spread) in spreads.items():
        noise = np.random.default_rng([zlib.crc32(name.encode()), seed]).standard_normal(out[name].shape)
        drawn = base * np.exp(spread * noise) if base else spread * noise
        out[name] = jnp.asarray(drawn.astype(out[name].dtype))
    for name, factor in factors.items():
        out[name] = (out[name] * factor).astype(out[name].dtype)
    return out
```

```python
from contextlib import ExitStack

import concourse.bass as bass
from concourse import mybir

F32 = mybir.dt.float32
F16 = mybir.dt.float16
BF16 = mybir.dt.bfloat16
I32 = mybir.dt.int32
U32 = mybir.dt.uint32
ALU = mybir.AluOpType
ACT = mybir.ActivationFunctionType
AX_X = mybir.AxisListType.X

P = 128
HEADS = 16
LN_EPS = 1e-5
DEN_EPS = 1e-6


def preln_linear_attention_moe(nc, x, wq, bq, wk, bk, wv, bv, wo, bo, Wr, W1, b1, W2, b2, out):
    B, N, D = x.shape
    E, _, F = W1.shape
    assert D == P and N % P == 0 and F % P == 0
    J = N // P
    T = B * J
    TOK = B * N
    HD = D // HEADS
    FC = F // P
    SLOT_TILES = T + E - 1
    RING = 4
    ROW = D + D + 4
    NV = D + 1
    ND = D + HEADS
    SKIP = 2 * TOK

    with ExitStack() as ctx:
        def sb(name, shape, dt=F32):
            return ctx.enter_context(nc.sbuf_tensor(name, shape, dt))

        def ps(name, shape, dt=F32):
            return ctx.enter_context(nc.psum_tensor(name, shape, dt))

        def sem(name):
            return ctx.enter_context(nc.semaphore(name))

        rows_dram = nc.dram_tensor("token_rows", [TOK, ROW], F32, kind="Internal").ap()

        x_sb = sb("x_sb", [P, T, D])
        wq_sb = sb("wq_sb", [P, D])
        wkv_sb = sb("wkv_sb", [P, 2 * D])
        wo_sb = sb("wo_sb", [P, D])
        wr_sb = sb("wr_sb", [P, E])
        w1_sb = sb("w1_sb", [P, E, F])
        w2_sb = sb("w2_sb", [P, E, FC, D])
        b1_rows = sb("b1_rows", [E * FC, P])
        b1_sb = sb("b1_sb", [P, E * FC])
        b2_sb = sb("b2_sb", [P, E * D])
        bias_in = sb("bias_in", [P, 4 * D])
        bias_hi = sb("bias_hi", [P, 4 * D], BF16)
        bias_mid = sb("bias_mid", [P, 4 * D], BF16)
        bias_lo = sb("bias_lo", [P, 4 * D], BF16)
        bias_r1 = sb("bias_r1", [P, 4 * D])
        bias_r2 = sb("bias_r2", [P, 4 * D])
        bias_p0 = sb("bias_p0", [P, 4 * D], BF16)
        bias_p1 = sb("bias_p1", [P, 4 * D], BF16)
        bias_rows = sb("bias_rows", [P, 4 * D], BF16)

        ident = sb("ident", [P, P])
        head_mask = sb("head_mask", [P, D])
        head_sel = sb("head_sel", [P, HEADS])
        before = sb("before", [P, P], F16)
        ones16 = sb("ones16", [P, P], F16)
        ones_bf = sb("ones_bf", [P, N], BF16)
        iota_lo = sb("iota_lo", [P, P], F16)
        expert_m = sb("expert_m", [P, J, E])
        iota_hi = sb("iota_hi", [P, SLOT_TILES])
        token_1 = sb("token_1", [P, T])
        tile_thr = sb("tile_thr", [P, E, T])
        tile_no = sb("tile_no", [1, SLOT_TILES, E])
        ones_e = sb("ones_e", [P, E])
        minus_half = sb("minus_half", [P, J])

        st1 = sb("st1", [P, T, 6])
        mv1 = sb("mv1", [P, T, 2])
        ve1 = sb("ve1", [P, T])
        nm1 = sb("nm1", [P, T])
        rs1 = sb("rs1", [P, T])
        nmr1 = sb("nmr1", [P, T])
        xn = sb("xn", [P, T, D])
        xnT = sb("xnT", [P, T, D])
        e_q = sb("e_q", [P, B, N])
        qT = sb("qT", [P, B, N])
        e_k = sb("e_k", [P, T, D])
        k_sb = sb("k_sb", [P, T, D])
        v_sb = sb("v_sb", [P, T, NV])
        kvd = sb("kvd", [P, B, ND])
        den = sb("den", [P, T, HEADS])
        zed = sb("zed", [P, T, HEADS])
        sc = sb("sc", [P, T, D])
        scT = sb("scT", [P, T, D])
        st2 = sb("st2", [P, T, 6])
        mv2 = sb("mv2", [P, T, 2])
        ve2 = sb("ve2", [P, T])
        nm2 = sb("nm2", [P, T])
        rs2 = sb("rs2", [P, T])
        rows = sb("rows", [P, T, ROW])
        hT = sb("hT", [P, T, D])
        lmax = sb("lmax", [P, T])
        lm = sb("lm", [P, T, E])
        pick = sb("pick", [P, T, E])
        first = sb("first", [P, T])
        onehot = sb("onehot", [P, T, E], F16)
        cum = sb("cum", [P, T + 1, E], F16)
        ex = sb("ex", [P, T, E])
        exsum = sb("exsum", [P, T])
        rk_m = sb("rk_m", [P, T, E])
        rank = sb("rank", [P, T], I32)
        rank_lo = sb("rank_lo", [P, T], I32)
        rank_lof = sb("rank_lof", [P, T])
        rank_hi = sb("rank_hi", [P, T], I32)
        lo_hot = sb("lo_hot", [P, T, P], F16)
        over = sb("over", [P, E, T])
        tiles_e = sb("tiles_e", [P, E])
        tiles_incl = sb("tiles_incl", [P, E])
        tiles_base = sb("tiles_base", [P, E])
        base_m = sb("base_m", [P, T, E])
        base_t = sb("base_t", [P, T])
        slot_hi = sb("slot_hi", [P, T])
        hi_hot = sb("hi_hot", [P, T, SLOT_TILES])
        hi_tok = sb("hi_tok", [P, T, SLOT_TILES], F16)
        past = sb("past", [1, SLOT_TILES, E])
        past_n = sb("past_n", [1, SLOT_TILES])
        tile_expert = sb("tile_expert", [1, SLOT_TILES], I32)
        gather_at = sb("gather_at", [P, SLOT_TILES], I32)
        padding = sb("padding", [P, SLOT_TILES])
        scatter_at = sb("scatter_at", [P, SLOT_TILES], I32)

        slots = sb("slots", [P, RING, ROW])
        tT = sb("tT", [P, RING, P])
        w1_st = sb("w1_st", [P, 2, F])
        w2_st = sb("w2_st", [P, 2, FC, D])
        b1_st = sb("b1_st", [P, 2, FC])
        hid = sb("hid", [P, 2, FC, P])
        yb = sb("yb", [P, RING, D])
        y_sb = sb("y_sb", [P, RING, D])

        bank = [ps(f"bank{i}", [P, 512]) for i in range(8)]
        xnT_ps = bank[0]
        att_ps = bank[0]
        q_ps = bank[1]
        kv_ps = [bank[2], bank[3]]
        ks_ps = bank[4]
        hT_ps = bank[4]
        nd_ps = [bank[5], bank[6]]
        scT_ps = bank[7]
        lg_ps = bank[7]
        rk_ps = bank[7]
        b1_ps = bank[5]
        cnt_ps = bank[7]
        perm_ps = bank[1]
        tT_ps = [bank[0], bank[4]]
        hid_ps = [bank[2], bank[3]]
        y_ps = [bank[5], bank[6]]

        x_in = [sem(f"x_in{b}") for b in range(B)]
        wq_in, wkv_in, bias_in_s, wo_in, wr_in = sem("wq_in"), sem("wkv_in"), sem("bias_in_s"), sem("wo_in"), sem("wr_in")
        b1_in, b2_in, w1_in, w2_in = sem("b1_in"), sem("b2_in"), sem("w1_in"), sem("w2_in")
        pool_set, pool_const = sem("pool_set"), sem("pool_const")
        dve_const, bias_ch, bias_done = sem("dve_const"), sem("bias_ch"), sem("bias_done")
        st1_s, mv1_s, ve1_s, rs1_s, nmr1_s, xn_s = sem("st1_s"), sem("mv1_s"), sem("ve1_s"), sem("rs1_s"), sem("nmr1_s"), sem("xn_s")
        xnT_mm, xnT_s = sem("xnT_mm"), sem("xnT_s")
        q_mm, eq_s, q_s = sem("q_mm"), sem("eq_s"), sem("q_s")
        kv_mm, ek_s, k_s, v_s = sem("kv_mm"), sem("ek_s"), sem("k_s"), sem("v_s")
        ks_mm, kvd_s = sem("ks_mm"), sem("kvd_s")
        nd_mm, den_s, zed_s, sc_s = sem("nd_mm"), sem("den_s"), sem("zed_s"), sem("sc_s")
        scT_mm, scT_s = sem("scT_mm"), sem("scT_s")
        att_mm, x1_s = sem("att_mm"), sem("x1_s")
        st2_s, mv2_s, ve2_s, rs2_s, h_s = sem("st2_s"), sem("mv2_s"), sem("ve2_s"), sem("rs2_s"), sem("h_s")
        hT_mm, hT_s = sem("hT_mm"), sem("hT_s")
        lg_mm, lmax_s, lm_s, pick_s, first_s, onehot_s, cum_s = (sem("lg_mm"), sem("lmax_s"), sem("lm_s"), sem("pick_s"),
                                                                sem("first_s"), sem("onehot_s"), sem("cum_s"))
        ex_s, exsum_s, prob_s = sem("ex_s"), sem("exsum_s"), sem("prob_s")
        rk_mm, rkm_s, rank_s, lo_s, lof_s, lohot_s = sem("rk_mm"), sem("rkm_s"), sem("rank_s"), sem("lo_s"), sem("lof_s"), sem("lohot_s")
        rows_out = sem("rows_out")
        cnt_mm, route_ch, tile_expert_s, hitok_s = sem("cnt_mm"), sem("route_ch"), sem("tile_expert_s"), sem("hitok_s")
        perm_mm, idx_s = sem("perm_mm"), sem("idx_s")
        b1_mm, b1_s = sem("b1_mm"), sem("b1_s")
        slots_in = [sem(f"slots_in{r}") for r in range(RING)]
        y_out = [sem(f"y_out{r}") for r in range(RING)]
        tT_mm, tT_s, w1_s, b1st_s, w2_s = sem("tT_mm"), sem("tT_s"), sem("w1_s"), sem("b1st_s"), sem("w2_s")
        hid_mm, hid_s, y_mm, yb_s, y_s = sem("hid_mm"), sem("hid_s"), sem("y_mm"), sem("yb_s"), sem("y_s")

        block = ctx.enter_context(nc.Block())

        x_v = x.rearrange("b (p j) d -> b p j d", j=J)
        rows_v = rows_dram.rearrange("(b p j) r -> b p j r", b=B, j=J)
        out_flat = out.rearrange("b n d -> (b n) d")

        def tiles(b):
            return slice(b * J, (b + 1) * J)

        @block.sync
        def _(sp):
            for b in range(B):
                sp.dma_start(x_sb[:, tiles(b), :], x_v[b]).then_inc(x_in[b], 16)
            sp.dma_start(wo_sb[:], wo).then_inc(wo_in, 16)
            sp.dma_start(wr_sb[:], Wr).then_inc(wr_in, 16)
            sp.dma_start(b1_rows[:], b1.rearrange("e (c p) -> (e c) p", p=P)).then_inc(b1_in, 16)
            for h in range(2):
                es = slice(h * E // 2, (h + 1) * E // 2)
                sp.dma_start(w1_sb[:, es, :], W1[es].rearrange("e d f -> d e f")).then_inc(w1_in, 16)
            for e in range(E):
                sp.dma_start(w2_sb[:, e], W2[e].rearrange("(c p) d -> p c d", p=P)).then_inc(w2_in, 16)
            sp.dma_start(b2_sb[:], b2.rearrange("e d -> (e d)").partition_broadcast(P)).then_inc(b2_in, 16)
            for b in range(B):
                sp.wait_ge(prob_s, b + 1)
                sp.wait_ge(h_s, J * (b + 1))
                sp.dma_start(rows_v[b], rows[:, tiles(b), :]).then_inc(rows_out, 16)
            for r in range(RING):
                sp.wait_ge(y_out[r], 16 * ((SLOT_TILES - r + RING - 1) // RING))

        @block.gpsimd
        def _(pool):
            n = [0]

            def cleared(ins):
                n[0] += 1
                ins.then_inc(pool_set, 1)
                pool.wait_ge(pool_set, n[0])

            def select(t, pattern, cm, op, fill, base=0):
                return pool.affine_select(out=t, in_=t, compare_op=op, fill=fill, base=base, pattern=pattern,
                                          channel_multiplier=cm)

            cleared(pool.memset(ident[:], 0.0))
            select(ident[:], [[-1, P]], 1, ALU.not_equal, 1.0).then_inc(pool_const, 1)
            pool.memset(minus_half[:], -0.5).then_inc(pool_const, 1)

            def ln_scale(b, mv_s, mv, ve_s, ve, nm, rs_s, rs):
                pool.wait_ge(mv_s, J * (b + 1))
                pool.tensor_scalar(ve[:, tiles(b)], mv[:, tiles(b), 1], LN_EPS, None, ALU.add).then_inc(ve_s, 1)
                pool.tensor_scalar(nm[:, tiles(b)], mv[:, tiles(b), 0], -1.0, None, ALU.mult).then_inc(ve_s, 1)
                pool.wait_ge(ve_s, 2 * (b + 1))
                pool.tensor_tensor(rs[:, tiles(b)], ve[:, tiles(b)], minus_half[:], ALU.pow).then_inc(rs_s, 1)
                pool.wait_ge(rs_s, b + 1)

            def ln1(b):
                ln_scale(b, mv1_s, mv1, ve1_s, ve1, nm1, rs1_s, rs1)
                pool.tensor_tensor(nmr1[:, tiles(b)], nm1[:, tiles(b)], rs1[:, tiles(b)], ALU.mult).then_inc(nmr1_s, 1)

            def ln2(b):
                ln_scale(b, mv2_s, mv2, ve2_s, ve2, nm2, rs2_s, rs2)
                for t in range(b * J, (b + 1) * J):
                    pool.tensor_scalar(rows[:, t, 0:D], rows[:, t, D:2 * D], nm2[:, t:t + 1], rs2[:, t:t + 1],
                                       ALU.add, ALU.mult).then_inc(h_s, 1)

            def lo_hots(b):
                pool.wait_ge(lof_s, b + 1)
                for t in range(b * J, (b + 1) * J):
                    pool.tensor_scalar(lo_hot[:, t, :], iota_lo[:], rank_lof[:, t:t + 1], None, ALU.is_equal)\
                        .then_inc(lohot_s, 1)

            ln1(0)
            cleared(pool.memset(head_mask[:], 1.0))
            hm = head_mask[:].rearrange("p (h e) -> p h e", e=HD)
            cleared(select(hm, [[-HD, HEADS], [0, HD]], 1, ALU.is_ge, 0.0))
            cleared(select(hm, [[HD, HEADS], [0, HD]], -1, ALU.is_ge, 0.0, base=HD - 1))
            cleared(pool.memset(head_sel[:], 1.0))
            cleared(select(head_sel[:], [[-HD, HEADS]], 1, ALU.is_ge, 0.0))
            select(head_sel[:], [[HD, HEADS]], -1, ALU.is_ge, 0.0, base=HD - 1).then_inc(pool_const, 1)
            ln1(1)
            cleared(pool.memset(before[:], 1.0))
            select(before[:], [[1, P]], -1, ALU.is_gt, 0.0).then_inc(pool_const, 1)
            pool.iota(expert_m[:], pattern=[[0, J], [1, E]], base=-E, channel_multiplier=0,
                      allow_small_or_imprecise_dtypes=True).then_inc(pool_const, 1)
            pool.iota(iota_lo[:], pattern=[[1, P]], base=0, channel_multiplier=0,
                      allow_small_or_imprecise_dtypes=True).then_inc(pool_const, 1)
            ln1(2)
            pool.iota(iota_hi[:], pattern=[[1, SLOT_TILES]], base=0, channel_multiplier=0,
                      allow_small_or_imprecise_dtypes=True).then_inc(pool_const, 1)
            pool.iota(token_1[:], pattern=[[N, B], [1, J]], base=1, channel_multiplier=J,
                      allow_small_or_imprecise_dtypes=True).then_inc(pool_const, 1)
            pool.iota(tile_thr[:], pattern=[[0, E], [P, T]], base=0, channel_multiplier=0,
                      allow_small_or_imprecise_dtypes=True).then_inc(pool_const, 1)
            pool.iota(tile_no[:], pattern=[[1, SLOT_TILES], [0, E]], base=0, channel_multiplier=0,
                      allow_small_or_imprecise_dtypes=True).then_inc(pool_const, 1)
            ln2(0)
            ln1(3)
            ln2(1)
            pool.wait_ge(pool_const, 6)
            lo_hots(0)
            ln2(2)
            lo_hots(1)
            ln2(3)
            lo_hots(2)
            lo_hots(3)

            pool.wait_ge(rows_out, 16 * B)
            pool.wait_ge(idx_s, 3)

            def gather(i):
                r = i % RING
                if i >= RING:
                    pool.wait_ge(tT_mm, i - RING + 1)
                    pool.wait_ge(y_s, i - RING + 1)
                pool.indirect_dma_start(
                    out=slots[:, r, :], out_offset=None, in_=rows_dram,
                    in_offset=bass.IndirectOffsetOnAxis(ap=gather_at[:, i:i + 1].bitcast(U32), axis=0),
                    bounds_check=TOK - 1, oob_is_err=False).then_inc(slots_in[r], 16)

            def scatter(i):
                r = i % RING
                pool.wait_ge(y_s, i + 1)
                pool.indirect_dma_start(
                    out=out_flat, out_offset=bass.IndirectOffsetOnAxis(ap=scatter_at[:, i:i + 1].bitcast(U32), axis=0),
                    in_=y_sb[:, r, :], in_offset=None, bounds_check=TOK - 1, oob_is_err=False)\
                    .then_inc(y_out[r], 16)

            for i in range(RING):
                gather(i)
            for i in range(SLOT_TILES):
                if i + RING < SLOT_TILES:
                    gather(i + RING)
                scatter(i)

        @block.scalar
        def _(act):
            act.dma_start(wq_sb[:], wq).then_inc(wq_in, 16)
            for i, bias in enumerate((bq, bk, bv, bo)):
                act.dma_start(bias_in[:, i * D:(i + 1) * D], bias.partition_broadcast(P)).then_inc(bias_in_s, 16)
            act.dma_start(wkv_sb[:, 0:D], wk).then_inc(wkv_in, 16)
            act.dma_start(wkv_sb[:, D:2 * D], wv).then_inc(wkv_in, 16)

            def normalise(b):
                act.wait_ge(x_in[b], 16)
                act.wait_ge(nmr1_s, b + 1)
                for t in range(b * J, (b + 1) * J):
                    act.activation(xn[:, t, :], x_sb[:, t, :], ACT.Identity, bias=nmr1[:, t:t + 1],
                                   scale=rs1[:, t:t + 1]).then_inc(xn_s, 1)

            def copy_xnT(b):
                act.wait_ge(xnT_mm, b + 1)
                act.copy(xnT[:, tiles(b), :], xnT_ps[:].rearrange("p (j d) -> p j d", j=J)).then_inc(xnT_s, 1)

            def exp_q(b):
                act.wait_ge(q_mm, b + 1)
                act.activation(e_q[:, b, :], q_ps[:], ACT.Exp, bias=-1.0).then_inc(eq_s, 1)

            def exp_k_copy_v(b):
                act.wait_ge(kv_mm, b + 1)
                for h in range(2):
                    ts = slice(b * J + 2 * h, b * J + 2 * h + 2)
                    kv = kv_ps[h][:].rearrange("p (j c) -> p j c", j=2)
                    act.activation(e_k[:, ts, :], kv[:, :, 0:D], ACT.Exp, bias=-1.0).then_inc(ek_s, 1)
                    act.copy(v_sb[:, ts, 0:D], kv[:, :, D:2 * D]).then_inc(v_s, 1)

            def copy_scT(b):
                act.wait_ge(scT_mm, b + 1)
                act.copy(scT[:, tiles(b), :], scT_ps[:].rearrange("p (j d) -> p j d", j=J)).then_inc(scT_s, 1)

            def copy_hT(b):
                act.wait_ge(hT_mm, b + 1)
                act.copy(hT[:, tiles(b), :], hT_ps[:].rearrange("p (j d) -> p j d", j=J)).then_inc(hT_s, 1)

            def exp_logits(b):
                act.wait_ge(lm_s, b + 1)
                act.activation(ex[:, tiles(b), :], lm[:, tiles(b), :], ACT.Exp).then_inc(ex_s, 1)

            normalise(0)
            for s in range(B + 2):
                if s < B:
                    copy_xnT(s)
                    exp_q(s)
                    if s + 1 < B:
                        normalise(s + 1)
                    exp_k_copy_v(s)
                if 1 <= s <= B:
                    copy_scT(s - 1)
                if s >= 2:
                    copy_hT(s - 2)
                    exp_logits(s - 2)
            act.wait_ge(b1_mm, 1)
            act.copy(b1_sb[:], b1_ps[:, 0:E * FC]).then_inc(b1_s, 1)
            act.preload_act_table(ACT.Gelu)

            def copy_tT(i, r, k):
                act.wait_ge(tT_mm, i + 1)
                act.copy(tT[:, r, :], tT_ps[k][:, 0:P]).then_inc(tT_s, 1)

            def gelu(i, k):
                act.wait_ge(hid_mm, i + 1)
                act.wait_ge(b1st_s, i + 1)
                for c in range(FC):
                    act.activation(hid[:, k, c, :], hid_ps[k][:, c * P:(c + 1) * P], ACT.Gelu,
                                   bias=b1_st[:, k, c:c + 1]).then_inc(hid_s, 1)

            copy_tT(0, 0, 0)
            copy_tT(1, 1, 1)
            gelu(0, 0)
            loops = (SLOT_TILES - 2) // RING
            with act.Fori(0, loops) as m:
                for r in range(RING):
                    i = m * RING + r
                    copy_tT(i + 2, (r + 2) % RING, r % 2)
                    gelu(i + 1, (r + 1) % 2)
            for i in range(loops * RING, SLOT_TILES):
                if i + 2 < SLOT_TILES:
                    copy_tT(i + 2, (i + 2) % RING, i % 2)
                if i + 1 < SLOT_TILES:
                    gelu(i + 1, (i + 1) % 2)

        @block.vector
        def _(dve):
            dve.memset(ones_bf[:], 1.0).then_inc(dve_const, 1)
            dve.memset(ones16[:], 1.0).then_inc(dve_const, 1)
            dve.memset(ones_e[:], 1.0).then_inc(dve_const, 1)
            dve.memset(v_sb[:, :, D:NV], 1.0).then_inc(dve_const, 1)
            dve.memset(rows[:, :, 2 * D:ROW], 0.0).then_inc(dve_const, 1)
            dve.memset(cum[:, 0, :], 0.0).then_inc(dve_const, 1)

            def moments(t0, src, st_s, st, mv_s, mv):
                for t in range(t0, t0 + J):
                    dve.bn_stats(st[:, t, :], src[:, t, :]).then_inc(st_s, 1)
                for t in range(t0, t0 + J):
                    dve.wait_ge(st_s, t + 1)
                    dve.bn_aggr(mv[:, t, :], st[:, t, :]).then_inc(mv_s, 1)

            def moments1(b):
                dve.wait_ge(x_in[b], 16)
                moments(b * J, x_sb, st1_s, st1, mv1_s, mv1)

            def bias_parts():
                c = [0]

                def step(ins):
                    c[0] += 1
                    ins.then_inc(bias_ch, 1)
                    dve.wait_ge(bias_ch, c[0])
                dve.wait_ge(bias_in_s, 64)
                step(dve.tensor_scalar(bias_in[:, 0:2 * D], bias_in[:, 0:2 * D], 1.0, None, ALU.add))
                step(dve.tensor_copy(bias_hi[:], bias_in[:]))
                step(dve.tensor_tensor(bias_r1[:], bias_in[:], bias_hi[:], ALU.subtract))
                step(dve.tensor_copy(bias_mid[:], bias_r1[:]))
                step(dve.tensor_tensor(bias_r2[:], bias_r1[:], bias_mid[:], ALU.subtract))
                step(dve.tensor_copy(bias_lo[:], bias_r2[:]))
                dve.wait_ge(pool_const, 1)
                step(dve.tensor_scalar(bias_p0[:], bias_hi[:], ident[:, 0:1], None, ALU.mult))
                step(dve.scalar_tensor_tensor(out=bias_p1[:], in0=bias_mid[:], scalar=ident[:, 1:2], in1=bias_p0[:],
                                              op0=ALU.mult, op1=ALU.add))
                dve.scalar_tensor_tensor(out=bias_rows[:], in0=bias_lo[:], scalar=ident[:, 2:3], in1=bias_p1[:],
                                         op0=ALU.mult, op1=ALU.add).then_inc(bias_done, 1)

            def feature_q(b):
                dve.wait_ge(eq_s, b + 1)
                dve.scalar_tensor_tensor(out=qT[:, b, :], in0=e_q[:, b, :], scalar=1.0, in1=q_ps[:], op0=ALU.min,
                                         op1=ALU.max).then_inc(q_s, 1)

            def feature_k(b):
                for h in range(2):
                    ts = slice(b * J + 2 * h, b * J + 2 * h + 2)
                    kv = kv_ps[h][:].rearrange("p (j c) -> p j c", j=2)
                    dve.wait_ge(v_s, 2 * b + h + 1)
                    dve.scalar_tensor_tensor(out=k_sb[:, ts, :], in0=e_k[:, ts, :], scalar=1.0, in1=kv[:, :, 0:D],
                                             op0=ALU.min, op1=ALU.max).then_inc(k_s, 1)

            def head_blocks(b):
                dve.wait_ge(ks_mm, b + 1)
                if b == 0:
                    dve.wait_ge(pool_const, 3)
                dve.tensor_tensor(kvd[:, b, 0:D], ks_ps[:, 0:D], head_mask[:], ALU.mult).then_inc(kvd_s, 1)
                dve.tensor_scalar(kvd[:, b, D:ND], head_sel[:], ks_ps[:, D:NV], None, ALU.mult).then_inc(kvd_s, 1)

            def attend(b):
                dve.wait_ge(nd_mm, b + 1)
                for h in range(2):
                    ts = slice(b * J + 2 * h, b * J + 2 * h + 2)
                    nd = nd_ps[h][:, 0:2 * ND].rearrange("p (j c) -> p j c", j=2)
                    dve.tensor_scalar(den[:, ts, :], nd[:, :, D:ND], DEN_EPS, None, ALU.add).then_inc(den_s, 1)
                dve.wait_ge(den_s, 2 * (b + 1))
                dve.reciprocal(zed[:, tiles(b), :], den[:, tiles(b), :]).then_inc(zed_s, 1)
                dve.wait_ge(zed_s, b + 1)
                for j in range(J):
                    t = b * J + j
                    num = nd_ps[j // 2][:, (j % 2) * ND:(j % 2) * ND + D].rearrange("p (h e) -> p h e", e=HD)
                    dve.tensor_tensor(sc[:, t, :].rearrange("p (h e) -> p h e", e=HD), num,
                                      zed[:, t, :].unsqueeze(2).broadcast_to([P, HEADS, HD]), ALU.mult)\
                        .then_inc(sc_s, 1)

            def residual(b):
                dve.wait_ge(att_mm, b + 1)
                dve.tensor_tensor(rows[:, tiles(b), D:2 * D], att_ps[:].rearrange("p (j d) -> p j d", j=J),
                                  x_sb[:, tiles(b), :], ALU.add).then_inc(x1_s, 1)
                dve.wait_ge(x1_s, b + 1)
                moments(b * J, rows[:, :, D:2 * D], st2_s, st2, mv2_s, mv2)

            def route(b):
                ts = tiles(b)
                lg = lg_ps[:, 0:J * E].rearrange("p (j e) -> p j e", j=J)
                dve.wait_ge(lg_mm, b + 1)
                dve.tensor_reduce(lmax[:, ts], lg, AX_X, ALU.max).then_inc(lmax_s, 1)
                dve.wait_ge(lmax_s, b + 1)
                dve.tensor_tensor(lm[:, ts, :], lg, lmax[:, ts].unsqueeze(2).broadcast_to([P, J, E]), ALU.subtract)\
                    .then_inc(lm_s, 1)
                dve.wait_ge(lm_s, b + 1)
                if b == 0:
                    dve.wait_ge(pool_const, 5)
                dve.scalar_tensor_tensor(out=pick[:, ts, :], in0=lm[:, ts, :], scalar=0.0, in1=expert_m[:],
                                         op0=ALU.is_equal, op1=ALU.mult).then_inc(pick_s, 1)
                dve.wait_ge(pick_s, b + 1)
                dve.tensor_reduce(first[:, ts], pick[:, ts, :], AX_X, ALU.min).then_inc(first_s, 1)
                dve.wait_ge(first_s, b + 1)
                dve.tensor_tensor(onehot[:, ts, :], expert_m[:], first[:, ts].unsqueeze(2).broadcast_to([P, J, E]),
                                  ALU.is_equal).then_inc(onehot_s, 1)
                dve.wait_ge(onehot_s, b + 1)
                for t in range(b * J, (b + 1) * J):
                    if t:
                        dve.wait_ge(cum_s, t)
                    dve.tensor_tensor(cum[:, t + 1, :], cum[:, t, :], onehot[:, t, :], ALU.add).then_inc(cum_s, 1)

            def top_probability(b):
                dve.wait_ge(ex_s, b + 1)
                dve.tensor_reduce(exsum[:, tiles(b)], ex[:, tiles(b), :], AX_X, ALU.add).then_inc(exsum_s, 1)
                dve.wait_ge(exsum_s, b + 1)
                dve.reciprocal(rows[:, tiles(b), 2 * D], exsum[:, tiles(b)]).then_inc(prob_s, 1)

            def ranks(b):
                ts = tiles(b)
                dve.wait_ge(rk_mm, b + 1)
                dve.tensor_tensor(rk_m[:, ts, :], rk_ps[:, 0:J * E].rearrange("p (j e) -> p j e", j=J),
                                  onehot[:, ts, :], ALU.mult).then_inc(rkm_s, 1)
                dve.wait_ge(rkm_s, b + 1)
                with nc.allow_low_precision(reason="whole numbers below 2**24"):
                    dve.tensor_reduce(rank[:, ts], rk_m[:, ts, :], AX_X, ALU.add).then_inc(rank_s, 1)
                dve.wait_ge(rank_s, b + 1)
                dve.tensor_scalar(rank_lo[:, ts], rank[:, ts], P - 1, None, ALU.bitwise_and).then_inc(lo_s, 1)
                dve.tensor_scalar(rank_hi[:, ts], rank[:, ts], P.bit_length() - 1, None, ALU.logical_shift_right)\
                    .then_inc(lo_s, 1)
                dve.wait_ge(lo_s, 2 * (b + 1))
                dve.tensor_copy(rank_lof[:, ts], rank_lo[:, ts]).then_inc(lof_s, 1)

            moments1(0)
            bias_parts()
            moments1(1)
            for s in range(B + 2):
                if 1 <= s <= B:
                    head_blocks(s - 1)
                if s < B:
                    feature_q(s)
                if s >= 3:
                    top_probability(s - 3)
                    ranks(s - 3)
                if 1 <= s <= B:
                    attend(s - 1)
                if s < B:
                    feature_k(s)
                if s + 2 < B:
                    moments1(s + 2)
                if 1 <= s <= B:
                    residual(s - 1)
                if s >= 2:
                    route(s - 2)
            ranks(B - 1)

            c = [0]

            def step(ins):
                c[0] += 1
                ins.then_inc(route_ch, 1)
                dve.wait_ge(route_ch, c[0])

            dve.wait_ge(pool_const, 10)
            dve.wait_ge(cnt_mm, 1)
            step(dve.tensor_tensor(over[:], cnt_ps[:, 0:E].unsqueeze(2).broadcast_to([P, E, T]), tile_thr[:], ALU.is_gt))
            step(dve.tensor_reduce(tiles_e[:], over[:], AX_X, ALU.add))
            step(dve.tensor_tensor_scan(tiles_incl[:], ones_e[:], tiles_e[:], 0.0, ALU.mult, ALU.add))
            step(dve.tensor_tensor(tiles_base[:], tiles_incl[:], tiles_e[:], ALU.subtract))
            step(dve.tensor_tensor(base_m[:], onehot[:], tiles_base[:].unsqueeze(1).broadcast_to([P, T, E]), ALU.mult))
            step(dve.tensor_reduce(base_t[:], base_m[:], AX_X, ALU.add))
            step(dve.tensor_tensor(slot_hi[:], base_t[:], rank_hi[:], ALU.add))
            step(dve.tensor_tensor(hi_hot[:], iota_hi[:].unsqueeze(1).broadcast_to([P, T, SLOT_TILES]),
                                   slot_hi[:].unsqueeze(2).broadcast_to([P, T, SLOT_TILES]), ALU.is_equal))
            dve.tensor_tensor(hi_tok[:], hi_hot[:], token_1[:].unsqueeze(2).broadcast_to([P, T, SLOT_TILES]), ALU.mult)\
                .then_inc(hitok_s, 1)
            step(dve.tensor_tensor(past[:], tile_no[:],
                                   tiles_incl[0:1, :].unsqueeze(1).broadcast_to([1, SLOT_TILES, E]), ALU.is_ge))
            step(dve.tensor_reduce(past_n[:], past[:], AX_X, ALU.add))
            dve.tensor_scalar(tile_expert[:], past_n[:], float(E - 1), None, ALU.min).then_inc(tile_expert_s, 1)
            top_probability(B - 1)

            dve.wait_ge(perm_mm, 1)
            dve.tensor_scalar(gather_at[:], perm_ps[:, 0:SLOT_TILES], -1.0, 0.0, ALU.add, ALU.max).then_inc(idx_s, 1)
            step(dve.tensor_scalar(padding[:], perm_ps[:, 0:SLOT_TILES], 0.0, float(SKIP), ALU.is_equal, ALU.mult))
            dve.scalar_tensor_tensor(out=scatter_at[:], in0=perm_ps[:, 0:SLOT_TILES], scalar=-1.0, in1=padding[:],
                                     op0=ALU.add, op1=ALU.add).then_inc(idx_s, 2)

            def expert_of(i):
                return dve.value_load(tile_expert[0:1, bass.ds(i, 1)] if not isinstance(i, int)
                                      else tile_expert[0:1, i:i + 1], min_val=0, max_val=E - 1)

            def stage_w1(i, k, old):
                e = expert_of(i)
                if old is not None:
                    dve.wait_ge(hid_mm, old + 1)
                    dve.wait_ge(hid_s, (old + 1) * FC)
                dve.tensor_copy(w1_st[:, k, :], w1_sb[:].rearrange("p e f -> p (e f)")[:, bass.ds(e * F, F)])\
                    .then_inc(w1_s, 1)
                dve.tensor_copy(b1_st[:, k, :], b1_sb[:, bass.ds(e * FC, FC)]).then_inc(b1st_s, 1)

            def stage_w2(i, k, old):
                e = expert_of(i)
                if old is not None:
                    dve.wait_ge(y_mm, old + 1)
                dve.tensor_copy(w2_st[:, k].rearrange("p c d -> p (c d)"),
                                w2_sb[:].rearrange("p e c d -> p (e c d)")[:, bass.ds(e * F, F)]).then_inc(w2_s, 1)

            def output_rows(i, r, k, old):
                e = expert_of(i)
                dve.wait_ge(y_mm, i + 1)
                dve.tensor_tensor(yb[:, r, :], y_ps[k][:, 0:D], b2_sb[:, bass.ds(e * D, D)], ALU.add).then_inc(yb_s, 1)
                dve.wait_ge(yb_s, i + 1)
                if old is not None:
                    dve.wait_ge(y_out[r], old)
                dve.scalar_tensor_tensor(out=y_sb[:, r, :], in0=yb[:, r, :], scalar=slots[:, r, 2 * D:2 * D + 1],
                                         in1=slots[:, r, D:2 * D], op0=ALU.mult, op1=ALU.add).then_inc(y_s, 1)

            dve.wait_ge(tile_expert_s, 1)
            dve.wait_ge(w1_in, 32)
            dve.wait_ge(b1_s, 1)
            for i in range(2):
                stage_w1(i, i, None)
            dve.wait_ge(w2_in, 16 * E)
            dve.wait_ge(b2_in, 16)
            for i in range(2):
                stage_w2(i, i, None)
            for i in range(RING):
                dve.wait_ge(slots_in[i], 16)
                stage_w1(i + 2, i % 2, i)
                output_rows(i, i, i % 2, None)
                stage_w2(i + 2, i % 2, i)
            loops = (SLOT_TILES - 2) // RING
            with dve.Fori(1, loops) as m:
                for r in range(RING):
                    i = m * RING + r
                    dve.wait_ge(slots_in[r], (m + 1) * 16)
                    stage_w1(i + 2, r % 2, i)
                    output_rows(i, r, r % 2, m * 16)
                    stage_w2(i + 2, r % 2, i)
            for i in range(loops * RING, SLOT_TILES):
                dve.wait_ge(slots_in[i % RING], (i // RING + 1) * 16)
                if i + 2 < SLOT_TILES:
                    stage_w1(i + 2, i % 2, i)
                output_rows(i, i % RING, i % 2, i // RING * 16)
                if i + 2 < SLOT_TILES:
                    stage_w2(i + 2, i % 2, i)

        @block.tensor
        def _(pe):
            def normalised_T(b):
                if b == 0:
                    pe.wait_ge(pool_const, 1)
                if b >= 2:
                    pe.wait_ge(x1_s, b - 1)
                for j in range(J):
                    pe.wait_ge(xn_s, b * J + j + 1)
                    last = pe.transpose(xnT_ps[:, j * P:(j + 1) * P], xn[:, b * J + j, :], ident[:])
                last.then_inc(xnT_mm, 1)

            def product_ks(b):
                pe.wait_ge(k_s, 2 * (b + 1))
                pe.wait_ge(v_s, 2 * (b + 1))
                if b == 0:
                    pe.wait_ge(dve_const, 6)
                if b >= 2:
                    pe.wait_ge(hT_s, b - 1)
                for j in range(J):
                    t = b * J + j
                    last = pe.matmul(ks_ps[:, 0:NV], k_sb[:, t, :], v_sb[:, t, :], start=j == 0, stop=j == J - 1)
                last.then_inc(ks_mm, 1)

            def product_q(b):
                pe.wait_ge(xnT_s, b + 1)
                if b == 0:
                    pe.wait_ge(wq_in, 16)
                else:
                    pe.wait_ge(q_s, b)
                pe.matmul(q_ps[:], wq_sb[:], xnT[:, tiles(b), :].rearrange("p j d -> p (j d)"), start=True, stop=False)
                if b == 0:
                    pe.wait_ge(bias_done, 1)
                pe.matmul(q_ps[:], bias_rows[:, 0:D], ones_bf[:], start=False, stop=True).then_inc(q_mm, 1)

            def product_kv(b):
                if b == 0:
                    pe.wait_ge(wkv_in, 32)
                else:
                    pe.wait_ge(k_s, 2 * b)
                    pe.wait_ge(v_s, 2 * b)
                for j in range(J):
                    dst = kv_ps[j // 2][:, (j % 2) * 2 * D:(j % 2 + 1) * 2 * D]
                    pe.matmul(dst, xnT[:, b * J + j, :], wkv_sb[:], start=True, stop=False)
                    last = pe.matmul(dst, ones_bf[:, 0:P], bias_rows[:, D:3 * D], start=False, stop=True)
                last.then_inc(kv_mm, 1)

            def product_nd(b):
                pe.wait_ge(q_s, b + 1)
                pe.wait_ge(kvd_s, 2 * (b + 1))
                if b >= 1:
                    pe.wait_ge(sc_s, J * b)
                for j in range(J):
                    last = pe.matmul(nd_ps[j // 2][:, (j % 2) * ND:(j % 2 + 1) * ND], qT[:, b, j * P:(j + 1) * P],
                                     kvd[:, b, :], start=True, stop=True)
                last.then_inc(nd_mm, 1)

            def scores_T(b):
                if b >= 2:
                    pe.wait_ge(rkm_s, b - 1)
                for j in range(J):
                    pe.wait_ge(sc_s, b * J + j + 1)
                    last = pe.transpose(scT_ps[:, j * P:(j + 1) * P], sc[:, b * J + j, :], ident[:])
                last.then_inc(scT_mm, 1)

            def rows_T(b):
                pe.wait_ge(kvd_s, 2 * min(b + 2, B))
                for j in range(J):
                    pe.wait_ge(h_s, b * J + j + 1)
                    last = pe.transpose(hT_ps[:, j * P:(j + 1) * P], rows[:, b * J + j, 0:D], ident[:])
                last.then_inc(hT_mm, 1)

            def product_o(b):
                pe.wait_ge(scT_s, b + 1)
                pe.wait_ge(xnT_s, min(b + 2, B))
                if b == 0:
                    pe.wait_ge(wo_in, 16)
                for j in range(J):
                    dst = att_ps[:, j * D:(j + 1) * D]
                    pe.matmul(dst, scT[:, b * J + j, :], wo_sb[:], start=True, stop=False)
                    last = pe.matmul(dst, ones_bf[:, 0:P], bias_rows[:, 3 * D:4 * D], start=False, stop=True)
                last.then_inc(att_mm, 1)

            def logits(b):
                pe.wait_ge(hT_s, b + 1)
                pe.wait_ge(scT_s, min(b + 2, B))
                if b == B - 1:
                    pe.wait_ge(rkm_s, b)
                if b == 0:
                    pe.wait_ge(wr_in, 16)
                for j in range(J):
                    last = pe.matmul(lg_ps[:, j * E:(j + 1) * E], hT[:, b * J + j, :], wr_sb[:], start=True, stop=True)
                last.then_inc(lg_mm, 1)

            def rank_sums(b):
                if b == 0:
                    pe.wait_ge(pool_const, 4)
                pe.wait_ge(onehot_s, b + 1)
                pe.wait_ge(cum_s, (b + 1) * J)
                flat = lambda t: t.rearrange("p j e -> p (j e)")
                pe.matmul(rk_ps[:, 0:J * E], before[:], flat(onehot[:, tiles(b), :]), start=True, stop=False)
                pe.matmul(rk_ps[:, 0:J * E], ones16[:], flat(cum[:, tiles(b), :]), start=False, stop=True)\
                    .then_inc(rk_mm, 1)

            for s in range(B + 2):
                if s < B:
                    normalised_T(s)
                if 1 <= s <= B:
                    product_ks(s - 1)
                if s >= 3:
                    rank_sums(s - 3)
                if s < B:
                    product_q(s)
                if 1 <= s <= B:
                    product_nd(s - 1)
                if s < B:
                    product_kv(s)
                if 1 <= s <= B:
                    scores_T(s - 1)
                if s >= 2:
                    rows_T(s - 2)
                if 1 <= s <= B:
                    product_o(s - 1)
                if s >= 2:
                    logits(s - 2)
            pe.wait_ge(b1_in, 16)
            pe.transpose(b1_ps[:, 0:E * FC], b1_rows[:], ident[0:E * FC, 0:E * FC]).then_inc(b1_mm, 1)
            rank_sums(B - 1)
            pe.wait_ge(rkm_s, B)
            pe.matmul(cnt_ps[:, 0:E], ones16[:], cum[:, T, :], start=True, stop=True).then_inc(cnt_mm, 1)
            pe.wait_ge(hitok_s, 1)
            pe.wait_ge(lohot_s, T)
            for t in range(T):
                last = pe.matmul(perm_ps[:, 0:SLOT_TILES], lo_hot[:, t, :], hi_tok[:, t, :], start=t == 0,
                                 stop=t == T - 1)
            last.then_inc(perm_mm, 1)

            def slots_T(i, r, k, turn):
                if not (isinstance(i, int) and i < 2):
                    pe.wait_ge(tT_s, i - 1)
                pe.wait_ge(slots_in[r], turn * 16)
                pe.transpose(tT_ps[k][:, 0:P], slots[:, r, 0:D], ident[:]).then_inc(tT_mm, 1)

            def hidden(i, r, k):
                pe.wait_ge(tT_s, i + 1)
                pe.wait_ge(w1_s, i + 1)
                if not (isinstance(i, int) and i < 2):
                    pe.wait_ge(hid_s, (i - 1) * FC)
                for c in range(FC):
                    last = pe.matmul(hid_ps[k][:, c * P:(c + 1) * P], w1_st[:, k, c * P:(c + 1) * P], tT[:, r, :],
                                     start=True, stop=True)
                last.then_inc(hid_mm, 1)

            def down(i, k):
                pe.wait_ge(hid_s, (i + 1) * FC)
                pe.wait_ge(w2_s, i + 1)
                if not (isinstance(i, int) and i < 2):
                    pe.wait_ge(yb_s, i - 1)
                for c in range(FC):
                    last = pe.matmul(y_ps[k][:, 0:D], hid[:, k, c, :], w2_st[:, k, c, :], start=c == 0, stop=c == FC - 1)
                last.then_inc(y_mm, 1)

            pe.wait_ge(b1_s, 1)
            slots_T(0, 0, 0, 1)
            slots_T(1, 1, 1, 1)
            hidden(0, 0, 0)
            for i in range(2):
                slots_T(i + 2, i + 2, i % 2, 1)
                hidden(i + 1, i + 1, (i + 1) % 2)
                down(i, i % 2)
            loops = (SLOT_TILES - 4) // RING
            with pe.Fori(0, loops) as m:
                for r in range(RING):
                    i = m * RING + r + 2
                    slots_T(i + 2, r, r % 2, m + 2)
                    hidden(i + 1, (r + 3) % RING, (r + 1) % 2)
                    down(i, r % 2)
            for i in range(loops * RING + 2, SLOT_TILES):
                if i + 2 < SLOT_TILES:
                    slots_T(i + 2, (i + 2) % RING, i % 2, (i + 2) // RING + 1)
                if i + 1 < SLOT_TILES:
                    hidden(i + 1, (i + 1) % RING, (i + 1) % 2)
                down(i, i % 2)


_INS = ['L0_attn_x', 'L0_attn_wq', 'L0_attn_bq', 'L0_attn_wk', 'L0_attn_bk', 'L0_attn_wv', 'L0_attn_bv', 'L0_attn_wo',
        'L0_attn_bo', 'L0_ffn_Wr', 'L0_ffn_W1', 'L0_ffn_b1', 'L0_ffn_W2', 'L0_ffn_b2']


def kernel(**inputs):
    import numpy as _np
    import concourse.bacc as _bacc
    from concourse import mybir as _mybir
    from concourse.bass_utils import run_bass_kernel_spmd as _run

    nc = _bacc.Bacc("TRN2", target_bir_lowering=False, num_devices=1)
    arrays, args = {}, []
    for name in _INS:
        a = _np.ascontiguousarray(inputs[name])
        arrays[f"in_{name}_dram"] = a
        args.append(nc.dram_tensor(f"in_{name}_dram", a.shape, _mybir.dt.from_np(a.dtype), kind="ExternalInput").ap())
    shape = inputs['L0_attn_x'].shape
    args.append(nc.dram_tensor("out_0_dram", shape, _mybir.dt.float32, kind="ExternalOutput").ap())
    preln_linear_attention_moe(nc, *args)
    r = _run(nc, [arrays], core_ids=[0])
    return r.results[0]["out_0_dram"]
```

```python
from contextlib import ExitStack

import concourse.bass as bass
from concourse import mybir

F32 = mybir.dt.float32
F16 = mybir.dt.float16
BF16 = mybir.dt.bfloat16
I32 = mybir.dt.int32
U32 = mybir.dt.uint32
ALU = mybir.AluOpType
ACT = mybir.ActivationFunctionType
AX_X = mybir.AxisListType.X

P = 128
HEADS = 16
LN_EPS = 1e-5
DEN_EPS = 1e-6
WARM_START = 14
WARM_ROUTING = 36


def preln_linear_attention_moe(nc, x, wq, bq, wk, bk, wv, bv, wo, bo, Wr, W1, b1, W2, b2, out):
    B, N, D = x.shape
    E, _, F = W1.shape
    assert D == P and N % P == 0 and F % P == 0
    J = N // P
    T = B * J
    TOK = B * N
    HD = D // HEADS
    FC = F // P
    SLOT_TILES = T + E - 1
    RING = 4
    PROB, NUMBER = D, D + 1
    TAIL = D + 4
    ROW = D + TAIL
    REGION = TOK + P
    NV = D + 1
    CNT = 64
    ND = D + HEADS
    SKIP = 2 * TOK
    FAR = (E + 1) * REGION

    with ExitStack() as ctx:
        def sb(name, shape, dt=F32):
            return ctx.enter_context(nc.sbuf_tensor(name, shape, dt))

        def ps(name, shape, dt=F32):
            return ctx.enter_context(nc.psum_tensor(name, shape, dt))

        def sem(name):
            return ctx.enter_context(nc.semaphore(name))

        rows_dram = nc.dram_tensor("routed_rows", [(E + 1) * REGION, ROW], F32, kind="Internal").ap()

        x_sb = sb("x_sb", [P, T, D])
        wq_sb = sb("wq_sb", [P, D])
        wkv_sb = sb("wkv_sb", [P, 2 * D])
        wo_sb = sb("wo_sb", [P, D])
        wr_sb = sb("wr_sb", [P, E])
        w1_sb = sb("w1_sb", [P, E, F])
        w2_sb = sb("w2_sb", [P, E, FC, D])
        b1_rows = sb("b1_rows", [E * FC, P])
        b1_sb = sb("b1_sb", [P, E * FC])
        b2_sb = sb("b2_sb", [P, E * D])
        bias_in = sb("bias_in", [P, 4 * D])
        bias_hi = sb("bias_hi", [P, 4 * D], BF16)
        bias_mid = sb("bias_mid", [P, 4 * D], BF16)
        bias_lo = sb("bias_lo", [P, 4 * D], BF16)
        bias_r1 = sb("bias_r1", [P, 4 * D])
        bias_r2 = sb("bias_r2", [P, 4 * D])
        bias_p0 = sb("bias_p0", [P, 4 * D], BF16)
        bias_p1 = sb("bias_p1", [P, 4 * D], BF16)
        bias_rows = sb("bias_rows", [P, 4 * D], BF16)

        ident = sb("ident", [P, P])
        head_mask = sb("head_mask", [P, D])
        head_sel = sb("head_sel", [P, HEADS])
        before = sb("before", [P, P], F16)
        ones16 = sb("ones16", [P, P], F16)
        ones_bf = sb("ones_bf", [P, N], BF16)
        region = sb("region", [P, J, E])
        region_row = sb("region_row", [1, E])
        tile_row0 = sb("tile_row0", [1, SLOT_TILES])
        tile_thr = sb("tile_thr", [1, E, T])
        tile_no = sb("tile_no", [1, SLOT_TILES, E])
        ones_e = sb("ones_e", [1, E])
        pad_rows = sb("pad_rows", [P, ROW])
        minus_half = sb("minus_half", [P, J])

        st1 = sb("st1", [P, T, 6])
        mv1 = sb("mv1", [P, T, 2])
        ve1 = sb("ve1", [P, T])
        nm1 = sb("nm1", [P, T])
        rs1 = sb("rs1", [P, T])
        nmr1 = sb("nmr1", [P, T])
        xn = sb("xn", [P, T, D])
        xnT = sb("xnT", [P, T, D])
        e_q = sb("e_q", [P, B, N])
        qT = sb("qT", [P, B, N])
        e_k = sb("e_k", [P, T, D])
        k_sb = sb("k_sb", [P, T, D])
        v_sb = sb("v_sb", [P, T, NV])
        kvd = sb("kvd", [P, B, ND])
        den = sb("den", [P, T, HEADS])
        zed = sb("zed", [P, T, HEADS])
        sc = sb("sc", [P, T, D])
        scT = sb("scT", [P, T, D])
        st2 = sb("st2", [P, T, 6])
        mv2 = sb("mv2", [P, T, 2])
        ve2 = sb("ve2", [P, T])
        nm2 = sb("nm2", [P, T])
        rs2 = sb("rs2", [P, T])
        rows = sb("rows", [P, T, ROW])
        hT = sb("hT", [P, T, D])
        lmax = sb("lmax", [P, T])
        lm = sb("lm", [P, T, E])
        pick = sb("pick", [P, T, E])
        first = sb("first", [P, T])
        onehot = sb("onehot", [P, T, E], F16)
        total = sb("total", [P, B, E], F16)
        ex = sb("ex", [P, T, E])
        exsum = sb("exsum", [P, T])
        rk_m = sb("rk_m", [P, T, E])
        rank = sb("rank", [P, T])
        slot = sb("slot", [P, T], I32)
        pad_at = sb("pad_at", [1, E], I32)
        over = sb("over", [1, E, T])
        tiles_e = sb("tiles_e", [1, E])
        tiles_incl = sb("tiles_incl", [1, E])
        past = sb("past", [1, SLOT_TILES, E])
        tile_expert = sb("tile_expert", [1, SLOT_TILES], I32)
        skip_e = sb("skip_e", [1, E - 1])
        skipped = sb("skipped", [1, SLOT_TILES, E - 1])
        skipped_n = sb("skipped_n", [1, SLOT_TILES])
        start_own = sb("start_own", [1, SLOT_TILES])
        bound = sb("bound", [1, SLOT_TILES])
        tile_start = sb("tile_start", [1, SLOT_TILES], I32)

        slot_h = sb("slot_h", [P, RING, D])
        slot_x = sb("slot_x", [P, RING, TAIL])
        tT = sb("tT", [P, RING, P])
        w1_st = sb("w1_st", [P, 2, F])
        w2_st = sb("w2_st", [P, 2, FC, D])
        b1_st = sb("b1_st", [P, 2, FC])
        hid = sb("hid", [P, 2, FC, P])
        yb = sb("yb", [P, RING, D])
        y_sb = sb("y_sb", [P, RING, D])

        pair23 = ps("bank23", [P, 2, 512])
        pair56 = ps("bank56", [P, 2, 512])
        bank = {i: ps(f"bank{i}", [P, 512]) for i in (0, 1, 4, 7)}
        bank |= {2: pair23[:, 0], 3: pair23[:, 1], 5: pair56[:, 0], 6: pair56[:, 1]}
        xnT_ps = bank[0]
        att_ps = bank[1]
        q_ps = bank[1]
        kv_ps = pair23[:].rearrange("p a (j c) -> p (a j) c", j=2)
        ks_ps = bank[4]
        hT_ps = bank[4]
        nd_ps = pair56[:].rearrange("p a (j c) -> p (a j) c", j=2)
        scT_ps = bank[7]
        lg_ps = bank[7]
        rk_ps = bank[7]
        b1_ps = bank[5]
        cnt_ps = bank[7]
        warm_ps = bank[0]
        tT_ps = [bank[0], bank[4]]
        hid_ps = [bank[2], bank[3]]
        y_ps = [bank[5], bank[6]]

        x_in = [sem(f"x_in{b}") for b in range(B)]
        wq_in, wkv_in, bias_in_s, wo_in, wr_in = sem("wq_in"), sem("wkv_in"), sem("bias_in_s"), sem("wo_in"), sem("wr_in")
        b1_in, b2_in, w1_in, w2_in = sem("b1_in"), sem("b2_in"), sem("w1_in"), sem("w2_in")
        pool_set, pool_const = sem("pool_set"), sem("pool_const")
        dve_const, bias_ch, bias_done = sem("dve_const"), sem("bias_ch"), sem("bias_done")
        st1_s, mv1_s, ve1_s, rs1_s, nmr1_s, xn_s = sem("st1_s"), sem("mv1_s"), sem("ve1_s"), sem("rs1_s"), sem("nmr1_s"), sem("xn_s")
        xnT_mm, xnT_s = sem("xnT_mm"), sem("xnT_s")
        q_mm, eq_s, q_s = sem("q_mm"), sem("eq_s"), sem("q_s")
        kv_mm, ek_s, k_s, v_s = sem("kv_mm"), sem("ek_s"), sem("k_s"), sem("v_s")
        ks_mm, kvd_s = sem("ks_mm"), sem("kvd_s")
        nd_mm, den_s, zed_s, sc_s = sem("nd_mm"), sem("den_s"), sem("zed_s"), sem("sc_s")
        scT_mm, scT_s = sem("scT_mm"), sem("scT_s")
        att_mm, x1_s = sem("att_mm"), sem("x1_s")
        st2_s, mv2_s, ve2_s, rs2_s, h_s = sem("st2_s"), sem("mv2_s"), sem("ve2_s"), sem("rs2_s"), sem("h_s")
        hT_mm, hT_s = sem("hT_mm"), sem("hT_s")
        lg_mm, lmax_s, lm_s, pick_s, first_s, onehot_s, total_s = (sem("lg_mm"), sem("lmax_s"), sem("lm_s"), sem("pick_s"),
                                                                  sem("first_s"), sem("onehot_s"), sem("total_s"))
        ex_s, exsum_s, prob_s = sem("ex_s"), sem("exsum_s"), sem("prob_s")
        rk_mm, rkm_s, rank_s, slot_s, number_s = sem("rk_mm"), sem("rkm_s"), sem("rank_s"), sem("slot_s"), sem("number_s")
        rows_out, pads_out = sem("rows_out"), sem("pads_out")
        cnt_mm, route_ch, pad_at_s, tile_expert_s, tile_start_s = (sem("cnt_mm"), sem("route_ch"), sem("pad_at_s"),
                                                                   sem("tile_expert_s"), sem("tile_start_s"))
        b1_mm, b1_s = sem("b1_mm"), sem("b1_s")
        slot_h_in = [sem(f"slot_h_in{r}") for r in range(RING)]
        slot_x_in = [sem(f"slot_x_in{r}") for r in range(RING)]
        y_out = [sem(f"y_out{r}") for r in range(RING)]
        tT_mm, tT_s, w1_s, b1st_s, w2_s = sem("tT_mm"), sem("tT_s"), sem("w1_s"), sem("b1st_s"), sem("w2_s")
        hid_mm, hid_s, y_mm, yb_s, y_s = sem("hid_mm"), sem("hid_s"), sem("y_mm"), sem("yb_s"), sem("y_s")

        block = ctx.enter_context(nc.Block())

        x_v = x.rearrange("b (p j) d -> b p j d", j=J)
        out_flat = out.rearrange("b n d -> (b n) d")

        def tiles(b):
            return slice(b * J, (b + 1) * J)

        def pad_experts(eng, experts):
            eng.wait_ge(number_s, 2)
            eng.wait_ge(pad_at_s, 1)
            for e in experts:
                at = eng.value_load(pad_at[0:1, e:e + 1], min_val=0, max_val=(E + 1) * REGION - P)
                eng.dma_start(rows_dram[bass.ds(at, P), :], pad_rows[:]).then_inc(pads_out, 16)

        @block.sync
        def _(sp):
            for b in range(B):
                sp.dma_start(x_sb[:, tiles(b), :], x_v[b]).then_inc(x_in[b], 16)
            sp.dma_start(wo_sb[:], wo).then_inc(wo_in, 16)
            sp.dma_start(wr_sb[:], Wr).then_inc(wr_in, 16)
            sp.dma_start(b1_rows[:], b1.rearrange("e (c p) -> (e c) p", p=P)).then_inc(b1_in, 16)
            for h in range(2):
                es = slice(h * E // 2, (h + 1) * E // 2)
                sp.dma_start(w1_sb[:, es, :], W1[es].rearrange("e d f -> d e f")).then_inc(w1_in, 16)
            for e in range(E):
                sp.dma_start(w2_sb[:, e], W2[e].rearrange("(c p) d -> p c d", p=P)).then_inc(w2_in, 16)
            sp.dma_start(b2_sb[:], b2.rearrange("e d -> (e d)").partition_broadcast(P)).then_inc(b2_in, 16)

            pad_experts(sp, range(E // 2))

            def first_row(i):
                col = tile_start[0:1, i:i + 1] if isinstance(i, int) else tile_start[0:1, bass.ds(i, 1)]
                return sp.value_load(col, min_val=0, max_val=(E + 1) * REGION - P)

            def load_h(i, r, reused):
                at = first_row(i)
                if reused:
                    sp.wait_ge(tT_mm, i - RING + 1)
                sp.dma_start(slot_h[:, r, :], rows_dram[bass.ds(at, P), 0:D]).then_inc(slot_h_in[r], 16)

            def load_x(i, r, old):
                at = first_row(i)
                if old is not None:
                    sp.wait_ge(y_out[r], old)
                sp.dma_start(slot_x[:, r, :], rows_dram[bass.ds(at, P), D:ROW]).then_inc(slot_x_in[r], 16)

            sp.wait_ge(tile_start_s, 1)
            sp.wait_ge(rows_out, 16 * T)
            sp.wait_ge(pads_out, 16 * E)
            for i in range(RING):
                load_h(i, i, False)
            for i in range(2):
                load_x(i, i, None)
            for i in range(2):
                load_x(i + 2, i + 2, None)
                load_h(i + RING, i, True)
            loops = (SLOT_TILES - RING - 2) // RING
            with sp.Fori(0, loops) as m:
                for r in range(RING):
                    i = m * RING + r + 2
                    load_x(i + 2, r, m * 16 + 16)
                    load_h(i + RING, (r + 2) % RING, True)
            for i in range(loops * RING + 2, SLOT_TILES - 2):
                load_x(i + 2, (i + 2) % RING, (i + 2) // RING * 16)
                if i + RING < SLOT_TILES:
                    load_h(i + RING, i % RING, True)
            for r in range(RING):
                sp.wait_ge(y_out[r], 16 * ((SLOT_TILES - r + RING - 1) // RING))

        @block.gpsimd
        def _(pool):
            n = [0]

            def cleared(ins):
                n[0] += 1
                ins.then_inc(pool_set, 1)
                pool.wait_ge(pool_set, n[0])

            def select(t, pattern, cm, op, fill, base=0):
                return pool.affine_select(out=t, in_=t, compare_op=op, fill=fill, base=base, pattern=pattern,
                                          channel_multiplier=cm)

            cleared(pool.memset(ident[:], 0.0))
            select(ident[:], [[-1, P]], 1, ALU.not_equal, 1.0).then_inc(pool_const, 1)
            pool.memset(minus_half[:], -0.5).then_inc(pool_const, 1)

            def ln_scale(b, mv_s, mv, ve_s, ve, nm, rs_s, rs):
                pool.wait_ge(mv_s, J * (b + 1))
                pool.tensor_scalar(ve[:, tiles(b)], mv[:, tiles(b), 1], LN_EPS, None, ALU.add).then_inc(ve_s, 1)
                pool.tensor_scalar(nm[:, tiles(b)], mv[:, tiles(b), 0], -1.0, None, ALU.mult).then_inc(ve_s, 1)
                pool.wait_ge(ve_s, 2 * (b + 1))
                pool.tensor_tensor(rs[:, tiles(b)], ve[:, tiles(b)], minus_half[:], ALU.pow).then_inc(rs_s, 1)
                pool.wait_ge(rs_s, b + 1)

            def ln1(b):
                ln_scale(b, mv1_s, mv1, ve1_s, ve1, nm1, rs1_s, rs1)
                pool.tensor_tensor(nmr1[:, tiles(b)], nm1[:, tiles(b)], rs1[:, tiles(b)], ALU.mult).then_inc(nmr1_s, 1)

            def ln2(b):
                if b == B - 1:
                    pool.wait_ge(ve2_s, 2 * (b + 1))
                    pool.tensor_tensor(rs2[:, tiles(b)], ve2[:, tiles(b)], minus_half[:], ALU.pow).then_inc(rs2_s, 1)
                    return
                ln_scale(b, mv2_s, mv2, ve2_s, ve2, nm2, rs2_s, rs2)
                for t in range(b * J, (b + 1) * J):
                    pool.tensor_scalar(rows[:, t, 0:D], rows[:, t, D:2 * D], nm2[:, t:t + 1], rs2[:, t:t + 1],
                                       ALU.add, ALU.mult).then_inc(h_s, 1)

            def scatter_rows(b):
                pool.wait_ge(slot_s, b + 1)
                pool.wait_ge(prob_s, b + 1)
                pool.wait_ge(h_s, J * (b + 1))
                for t in range(b * J, (b + 1) * J):
                    pool.indirect_dma_start(
                        out=rows_dram, out_offset=bass.IndirectOffsetOnAxis(ap=slot[:, t:t + 1].bitcast(U32), axis=0),
                        in_=rows[:, t, :], in_offset=None, bounds_check=(E + 1) * REGION - 1, oob_is_err=False)\
                        .then_inc(rows_out, 16)

            def scatter_output(i):
                r = i % RING
                pool.wait_ge(y_s, i + 1)
                pool.indirect_dma_start(
                    out=out_flat,
                    out_offset=bass.IndirectOffsetOnAxis(ap=slot_x[:, r, NUMBER:NUMBER + 1].bitcast(U32), axis=0),
                    in_=y_sb[:, r, :], in_offset=None, bounds_check=TOK - 1, oob_is_err=False)\
                    .then_inc(y_out[r], 16)

            ln1(0)
            cleared(pool.memset(head_mask[:], 1.0))
            hm = head_mask[:].rearrange("p (h e) -> p h e", e=HD)
            cleared(select(hm, [[-HD, HEADS], [0, HD]], 1, ALU.is_ge, 0.0))
            cleared(select(hm, [[HD, HEADS], [0, HD]], -1, ALU.is_ge, 0.0, base=HD - 1))
            cleared(pool.memset(head_sel[:], 1.0))
            cleared(select(head_sel[:], [[-HD, HEADS]], 1, ALU.is_ge, 0.0))
            select(head_sel[:], [[HD, HEADS]], -1, ALU.is_ge, 0.0, base=HD - 1).then_inc(pool_const, 1)
            ln1(1)
            cleared(pool.memset(before[:], 1.0))
            select(before[:], [[1, P]], -1, ALU.is_gt, 0.0).then_inc(pool_const, 1)
            pool.iota(region[:], pattern=[[0, J], [-1, E]], base=E, channel_multiplier=0,
                      allow_small_or_imprecise_dtypes=True).then_inc(pool_const, 1)
            ln1(2)
            ln1(3)
            pool.wait_ge(dve_const, 6)
            pool.iota(rows[:, :, D + NUMBER].bitcast(I32), pattern=[[N, B], [1, J]], base=0, channel_multiplier=J)\
                .then_inc(number_s, 1)
            pool.iota(pad_rows[:, D + NUMBER:D + NUMBER + 1].bitcast(I32), pattern=[[0, 1]], base=SKIP,
                      channel_multiplier=0).then_inc(number_s, 1)
            pool.iota(region_row[:], pattern=[[-REGION, E]], base=E * REGION, channel_multiplier=0,
                      allow_small_or_imprecise_dtypes=True).then_inc(pool_const, 1)
            pool.iota(tile_row0[:], pattern=[[P, SLOT_TILES]], base=E * REGION, channel_multiplier=0,
                      allow_small_or_imprecise_dtypes=True).then_inc(pool_const, 1)
            pool.iota(tile_thr[:], pattern=[[0, E], [P, T]], base=0, channel_multiplier=0,
                      allow_small_or_imprecise_dtypes=True).then_inc(pool_const, 1)
            pool.iota(tile_no[:], pattern=[[1, SLOT_TILES], [0, E]], base=0, channel_multiplier=0,
                      allow_small_or_imprecise_dtypes=True).then_inc(pool_const, 1)
            pool.wait_ge(number_s, 1)
            ln2(0)
            ln2(1)
            scatter_rows(0)
            ln2(2)
            scatter_rows(1)
            ln2(3)
            scatter_rows(2)
            scatter_rows(3)
            for i in range(SLOT_TILES):
                scatter_output(i)

        @block.scalar
        def _(act):
            act.dma_start(wq_sb[:], wq).then_inc(wq_in, 16)
            for i, bias in enumerate((bq, bk, bv, bo)):
                act.dma_start(bias_in[:, i * D:(i + 1) * D], bias.partition_broadcast(P)).then_inc(bias_in_s, 16)
            act.dma_start(wkv_sb[:, 0:D], wk).then_inc(wkv_in, 16)
            act.dma_start(wkv_sb[:, D:2 * D], wv).then_inc(wkv_in, 16)

            def normalise(b):
                act.wait_ge(x_in[b], 16)
                act.wait_ge(nmr1_s, b + 1)
                for t in range(b * J, (b + 1) * J):
                    act.activation(xn[:, t, :], x_sb[:, t, :], ACT.Identity, bias=nmr1[:, t:t + 1],
                                   scale=rs1[:, t:t + 1]).then_inc(xn_s, 1)

            def copy_xnT(b):
                act.wait_ge(xnT_mm, b + 1)
                act.copy(xnT[:, tiles(b), :], xnT_ps[:].rearrange("p (j d) -> p j d", j=J)).then_inc(xnT_s, 1)

            def exp_q(b):
                act.wait_ge(q_mm, b + 1)
                act.activation(e_q[:, b, :], q_ps[:], ACT.Exp, bias=-1.0).then_inc(eq_s, 1)

            def exp_k_copy_v(b):
                for h in range(2):
                    act.wait_ge(kv_mm, 2 * b + h + 1)
                    ts = slice(b * J + 2 * h, b * J + 2 * h + 2)
                    kv = kv_ps[:, 2 * h:2 * h + 2, :]
                    act.activation(e_k[:, ts, :], kv[:, :, 0:D], ACT.Exp, bias=-1.0).then_inc(ek_s, 1)
                    act.copy(v_sb[:, ts, 0:D], kv[:, :, D:2 * D]).then_inc(v_s, 1)

            def copy_scT(b):
                act.wait_ge(scT_mm, b + 1)
                act.copy(scT[:, tiles(b), :], scT_ps[:].rearrange("p (j d) -> p j d", j=J)).then_inc(scT_s, 1)

            def copy_hT(b):
                act.wait_ge(hT_mm, b + 1)
                act.copy(hT[:, tiles(b), :], hT_ps[:].rearrange("p (j d) -> p j d", j=J)).then_inc(hT_s, 1)

            def exp_logits(b):
                act.wait_ge(lm_s, b + 1)
                act.activation(ex[:, tiles(b), :], lm[:, tiles(b), :], ACT.Exp).then_inc(ex_s, 1)

            normalise(0)
            for s in range(B + 2):
                if s < B:
                    copy_xnT(s)
                    exp_q(s)
                    if s + 1 < B:
                        normalise(s + 1)
                if s >= 2:
                    copy_hT(s - 2)
                if s < B:
                    exp_k_copy_v(s)
                if 1 <= s <= B:
                    copy_scT(s - 1)
                if s >= 2:
                    exp_logits(s - 2)
            act.wait_ge(b1_mm, 1)
            act.copy(b1_sb[:], b1_ps[:, 0:E * FC]).then_inc(b1_s, 1)
            act.preload_act_table(ACT.Gelu)
            pad_experts(act, range(E // 2, E))

            def copy_tT(i, r, k):
                act.wait_ge(tT_mm, i + 1)
                act.copy(tT[:, r, :], tT_ps[k][:, 0:P]).then_inc(tT_s, 1)

            def gelu(i, k):
                act.wait_ge(hid_mm, i + 1)
                act.wait_ge(b1st_s, i + 1)
                for c in range(FC):
                    act.activation(hid[:, k, c, :], hid_ps[k][:, c * P:(c + 1) * P], ACT.Gelu,
                                   bias=b1_st[:, k, c:c + 1]).then_inc(hid_s, 1)

            copy_tT(0, 0, 0)
            copy_tT(1, 1, 1)
            gelu(0, 0)
            loops = (SLOT_TILES - 2) // RING
            with act.Fori(0, loops) as m:
                for r in range(RING):
                    i = m * RING + r
                    copy_tT(i + 2, (r + 2) % RING, r % 2)
                    gelu(i + 1, (r + 1) % 2)
            for i in range(loops * RING, SLOT_TILES):
                if i + 2 < SLOT_TILES:
                    copy_tT(i + 2, (i + 2) % RING, i % 2)
                if i + 1 < SLOT_TILES:
                    gelu(i + 1, (i + 1) % 2)

        @block.vector
        def _(dve):
            dve.memset(ones_bf[:], 1.0).then_inc(dve_const, 1)
            dve.memset(ones16[:], 1.0).then_inc(dve_const, 1)
            dve.memset(ones_e[:], 1.0).then_inc(dve_const, 1)
            dve.memset(v_sb[:, :, D:NV], 1.0).then_inc(dve_const, 1)
            dve.memset(rows[:, :, 2 * D:ROW], 0.0).then_inc(dve_const, 1)
            dve.memset(pad_rows[:], 0.0).then_inc(dve_const, 1)

            def moments(t0, src, st_s, st, mv_s, mv):
                for t in range(t0, t0 + J):
                    dve.bn_stats(st[:, t, :], src[:, t, :]).then_inc(st_s, 1)
                for t in range(t0, t0 + J):
                    dve.wait_ge(st_s, t + 1)
                    dve.bn_aggr(mv[:, t, :], st[:, t, :]).then_inc(mv_s, 1)

            def moments1(b):
                dve.wait_ge(x_in[b], 16)
                moments(b * J, x_sb, st1_s, st1, mv1_s, mv1)

            def bias_parts():
                c = [0]

                def step(ins):
                    c[0] += 1
                    ins.then_inc(bias_ch, 1)
                    dve.wait_ge(bias_ch, c[0])
                dve.wait_ge(bias_in_s, 64)
                step(dve.tensor_scalar(bias_in[:, 0:2 * D], bias_in[:, 0:2 * D], 1.0, None, ALU.add))
                step(dve.tensor_copy(bias_hi[:], bias_in[:]))
                step(dve.tensor_tensor(bias_r1[:], bias_in[:], bias_hi[:], ALU.subtract))
                step(dve.tensor_copy(bias_mid[:], bias_r1[:]))
                step(dve.tensor_tensor(bias_r2[:], bias_r1[:], bias_mid[:], ALU.subtract))
                step(dve.tensor_copy(bias_lo[:], bias_r2[:]))
                dve.wait_ge(pool_const, 1)
                step(dve.tensor_scalar(bias_p0[:], bias_hi[:], ident[:, 0:1], None, ALU.mult))
                step(dve.scalar_tensor_tensor(out=bias_p1[:], in0=bias_mid[:], scalar=ident[:, 1:2], in1=bias_p0[:],
                                              op0=ALU.mult, op1=ALU.add))
                dve.scalar_tensor_tensor(out=bias_rows[:], in0=bias_lo[:], scalar=ident[:, 2:3], in1=bias_p1[:],
                                         op0=ALU.mult, op1=ALU.add).then_inc(bias_done, 1)

            def feature_q(b):
                dve.wait_ge(eq_s, b + 1)
                dve.scalar_tensor_tensor(out=qT[:, b, :], in0=e_q[:, b, :], scalar=1.0, in1=q_ps[:], op0=ALU.min,
                                         op1=ALU.max).then_inc(q_s, 1)

            def feature_k(b):
                for h in range(2):
                    ts = slice(b * J + 2 * h, b * J + 2 * h + 2)
                    kv = kv_ps[:, 2 * h:2 * h + 2, :]
                    dve.wait_ge(v_s, 2 * b + h + 1)
                    dve.scalar_tensor_tensor(out=k_sb[:, ts, :], in0=e_k[:, ts, :], scalar=1.0, in1=kv[:, :, 0:D],
                                             op0=ALU.min, op1=ALU.max).then_inc(k_s, 1)

            def head_blocks(b):
                dve.wait_ge(ks_mm, b + 1)
                if b == 0:
                    dve.wait_ge(pool_const, 3)
                dve.tensor_tensor(kvd[:, b, 0:D], ks_ps[:, 0:D], head_mask[:], ALU.mult).then_inc(kvd_s, 1)
                dve.tensor_scalar(kvd[:, b, D:ND], head_sel[:], ks_ps[:, D:NV], None, ALU.mult).then_inc(kvd_s, 1)

            def attend(b):
                dve.wait_ge(nd_mm, b + 1)
                dve.tensor_scalar(den[:, tiles(b), :], nd_ps[:, :, D:ND], DEN_EPS, None, ALU.add).then_inc(den_s, 1)
                dve.wait_ge(den_s, b + 1)
                dve.reciprocal(zed[:, tiles(b), :], den[:, tiles(b), :]).then_inc(zed_s, 1)
                dve.wait_ge(zed_s, b + 1)
                dve.tensor_tensor(sc[:, tiles(b), :].rearrange("p j (h e) -> p j h e", e=HD),
                                  nd_ps[:, :, 0:D].rearrange("p j (h e) -> p j h e", e=HD),
                                  zed[:, tiles(b), :].unsqueeze(3).broadcast_to([P, J, HEADS, HD]), ALU.mult)\
                    .then_inc(sc_s, 1)

            def residual(b):
                dve.wait_ge(att_mm, b + 1)
                dve.tensor_tensor(rows[:, tiles(b), D:2 * D], att_ps[:].rearrange("p (j d) -> p j d", j=J),
                                  x_sb[:, tiles(b), :], ALU.add).then_inc(x1_s, 1)
                dve.wait_ge(x1_s, b + 1)
                moments(b * J, rows[:, :, D:2 * D], st2_s, st2, mv2_s, mv2)

            def last_ln2(b):
                dve.wait_ge(mv2_s, J * (b + 1))
                dve.tensor_scalar(ve2[:, tiles(b)], mv2[:, tiles(b), 1], LN_EPS, None, ALU.add).then_inc(ve2_s, 1)
                dve.tensor_scalar(nm2[:, tiles(b)], mv2[:, tiles(b), 0], -1.0, None, ALU.mult).then_inc(ve2_s, 1)
                dve.wait_ge(ve2_s, 2 * (b + 1))
                dve.wait_ge(rs2_s, b + 1)
                for t in range(b * J, (b + 1) * J):
                    dve.tensor_scalar(rows[:, t, 0:D], rows[:, t, D:2 * D], nm2[:, t:t + 1], rs2[:, t:t + 1],
                                      ALU.add, ALU.mult).then_inc(h_s, 1)

            def route(b):
                ts = tiles(b)
                lg = lg_ps[:, 0:J * E].rearrange("p (j e) -> p j e", j=J)
                dve.wait_ge(lg_mm, b + 1)
                dve.tensor_reduce(lmax[:, ts], lg, AX_X, ALU.max).then_inc(lmax_s, 1)
                dve.wait_ge(lmax_s, b + 1)
                dve.tensor_tensor(lm[:, ts, :], lg, lmax[:, ts].unsqueeze(2).broadcast_to([P, J, E]), ALU.subtract)\
                    .then_inc(lm_s, 1)
                dve.wait_ge(lm_s, b + 1)
                if b == 0:
                    dve.wait_ge(pool_const, 5)
                dve.scalar_tensor_tensor(out=pick[:, ts, :], in0=lm[:, ts, :], scalar=0.0, in1=region[:],
                                         op0=ALU.is_equal, op1=ALU.mult).then_inc(pick_s, 1)
                dve.wait_ge(pick_s, b + 1)
                dve.tensor_reduce(first[:, ts], pick[:, ts, :], AX_X, ALU.max).then_inc(first_s, 1)
                dve.wait_ge(first_s, b + 1)
                dve.tensor_tensor(onehot[:, ts, :], region[:], first[:, ts].unsqueeze(2).broadcast_to([P, J, E]),
                                  ALU.is_equal).then_inc(onehot_s, 1)
                dve.wait_ge(onehot_s, b + 1)
                with nc.allow_low_precision(reason="counts up to the tiles of a batch"):
                    dve.tensor_reduce(total[:, b, :], onehot[:, ts, :].rearrange("p j e -> p e j"), AX_X, ALU.add)\
                        .then_inc(total_s, 1)

            def top_probability(b):
                dve.wait_ge(ex_s, b + 1)
                dve.tensor_reduce(exsum[:, tiles(b)], ex[:, tiles(b), :], AX_X, ALU.add).then_inc(exsum_s, 1)
                dve.wait_ge(exsum_s, b + 1)
                dve.reciprocal(rows[:, tiles(b), 2 * D], exsum[:, tiles(b)]).then_inc(prob_s, 1)

            def slots(b):
                ts = tiles(b)
                if b < B - 1:
                    dve.wait_ge(rk_mm, b + 1)
                dve.tensor_tensor(rk_m[:, ts, :], rk_ps[:, 0:J * E].rearrange("p (j e) -> p j e", j=J),
                                  onehot[:, ts, :], ALU.mult).then_inc(rkm_s, 1)
                dve.wait_ge(rkm_s, b + 1)
                dve.tensor_reduce(rank[:, ts], rk_m[:, ts, :], AX_X, ALU.add).then_inc(rank_s, 1)
                dve.wait_ge(rank_s, b + 1)
                dve.scalar_tensor_tensor(out=slot[:, ts], in0=first[:, ts], scalar=float(REGION), in1=rank[:, ts],
                                         op0=ALU.mult, op1=ALU.add).then_inc(slot_s, 1)

            moments1(0)
            bias_parts()
            for b in range(1, B):
                moments1(b)
            for s in range(B + 2):
                if 1 <= s <= B:
                    head_blocks(s - 1)
                if s < B:
                    feature_q(s)
                if 3 <= s <= B:
                    top_probability(s - 3)
                    slots(s - 3)
                if 1 <= s <= B:
                    attend(s - 1)
                if s < B:
                    feature_k(s)
                if s >= 2:
                    route(s - 2)
                if 1 <= s <= B:
                    residual(s - 1)
                if s == B:
                    top_probability(B - 2)
                    slots(B - 2)
                    last_ln2(B - 1)
            top_probability(B - 1)

            c = [0]

            def step(ins):
                c[0] += 1
                ins.then_inc(route_ch, 1)
                dve.wait_ge(route_ch, c[0])

            dve.wait_ge(pool_const, 9)
            dve.wait_ge(cnt_mm, 1)
            cnt = cnt_ps[0:1, CNT:CNT + E]
            dve.tensor_tensor(pad_at[:], cnt, region_row[:], ALU.add).then_inc(pad_at_s, 1)
            slots(B - 1)
            step(dve.tensor_tensor(over[:], cnt.unsqueeze(2).broadcast_to([1, E, T]), tile_thr[:], ALU.is_gt))
            step(dve.tensor_reduce(tiles_e[:], over[:], AX_X, ALU.add))
            step(dve.tensor_tensor_scan(tiles_incl[:], ones_e[:], tiles_e[:], 0.0, ALU.mult, ALU.add))
            step(dve.tensor_tensor(past[:], tile_no[:],
                                   tiles_incl[:].unsqueeze(1).broadcast_to([1, SLOT_TILES, E]), ALU.is_ge))
            with nc.allow_low_precision(reason="whole numbers up to the number of experts"):
                dve.tensor_reduce(tile_expert[:], past[:, :, 0:E - 1], AX_X, ALU.add).then_inc(tile_expert_s, 1)
            step(dve.tensor_scalar(skip_e[:], tiles_e[:, 0:E - 1], float(-P), float(-REGION), ALU.mult, ALU.add))
            step(dve.tensor_tensor(skipped[:], past[:, :, 0:E - 1],
                                   skip_e[:].unsqueeze(1).broadcast_to([1, SLOT_TILES, E - 1]), ALU.mult))
            step(dve.tensor_reduce(skipped_n[:], skipped[:], AX_X, ALU.add))
            step(dve.tensor_tensor(start_own[:], skipped_n[:], tile_row0[:], ALU.add))
            step(dve.tensor_scalar(bound[:], past[:, :, E - 2], float(-FAR), cnt_ps[0:1, CNT + E - 1:CNT + E],
                                   ALU.mult, ALU.add))
            dve.scalar_tensor_tensor(out=tile_start[:], in0=bound[:], scalar=float(FAR + REGION), in1=start_own[:],
                                     op0=ALU.add, op1=ALU.min).then_inc(tile_start_s, 1)

            def expert_of(i):
                return dve.value_load(tile_expert[0:1, bass.ds(i, 1)] if not isinstance(i, int)
                                      else tile_expert[0:1, i:i + 1], min_val=0, max_val=E - 1)

            def stage_w1(i, k, old):
                e = expert_of(i)
                if old is not None:
                    dve.wait_ge(hid_mm, old + 1)
                    dve.wait_ge(hid_s, (old + 1) * FC)
                dve.tensor_copy(w1_st[:, k, :], w1_sb[:].rearrange("p e f -> p (e f)")[:, bass.ds(e * F, F)])\
                    .then_inc(w1_s, 1)
                dve.tensor_copy(b1_st[:, k, :], b1_sb[:, bass.ds(e * FC, FC)]).then_inc(b1st_s, 1)

            def stage_w2(i, k, old):
                e = expert_of(i)
                if old is not None:
                    dve.wait_ge(y_mm, old + 1)
                dve.tensor_copy(w2_st[:, k].rearrange("p c d -> p (c d)"),
                                w2_sb[:].rearrange("p e c d -> p (e c d)")[:, bass.ds(e * F, F)]).then_inc(w2_s, 1)

            def output_rows(i, r, k, old):
                e = expert_of(i)
                dve.wait_ge(y_mm, i + 1)
                if old is not None:
                    dve.wait_ge(y_out[r], old)
                dve.tensor_tensor(yb[:, r, :], y_ps[k][:, 0:D], b2_sb[:, bass.ds(e * D, D)], ALU.add).then_inc(yb_s, 1)
                dve.wait_ge(yb_s, i + 1)
                dve.scalar_tensor_tensor(out=y_sb[:, r, :], in0=yb[:, r, :], scalar=slot_x[:, r, PROB:PROB + 1],
                                         in1=slot_x[:, r, 0:D], op0=ALU.mult, op1=ALU.add).then_inc(y_s, 1)

            dve.wait_ge(tile_expert_s, 1)
            dve.wait_ge(w1_in, 32)
            dve.wait_ge(b1_s, 1)
            for i in range(2):
                stage_w1(i, i, None)
            dve.wait_ge(w2_in, 16 * E)
            dve.wait_ge(b2_in, 16)
            for i in range(2):
                stage_w2(i, i, None)
            for i in range(RING):
                dve.wait_ge(slot_x_in[i], 16)
                stage_w1(i + 2, i % 2, i)
                output_rows(i, i, i % 2, None)
                stage_w2(i + 2, i % 2, i)
            loops = (SLOT_TILES - 2) // RING
            with dve.Fori(1, loops) as m:
                for r in range(RING):
                    i = m * RING + r
                    dve.wait_ge(slot_x_in[r], (m + 1) * 16)
                    stage_w1(i + 2, r % 2, i)
                    output_rows(i, r, r % 2, m * 16)
                    stage_w2(i + 2, r % 2, i)
            for i in range(loops * RING, SLOT_TILES):
                dve.wait_ge(slot_x_in[i % RING], (i // RING + 1) * 16)
                if i + 2 < SLOT_TILES:
                    stage_w1(i + 2, i % 2, i)
                output_rows(i, i % RING, i % 2, i // RING * 16)
                if i + 2 < SLOT_TILES:
                    stage_w2(i + 2, i % 2, i)

        @block.tensor
        def _(pe):
            def normalised_T(b):
                if b == 0:
                    pe.wait_ge(pool_const, 1)
                else:
                    pe.wait_ge(xnT_s, b)
                for j in range(J):
                    pe.wait_ge(xn_s, b * J + j + 1)
                    last = pe.transpose(xnT_ps[:, j * P:(j + 1) * P], xn[:, b * J + j, :], ident[:])
                last.then_inc(xnT_mm, 1)

            def product_ks(b):
                pe.wait_ge(k_s, 2 * (b + 1))
                pe.wait_ge(v_s, 2 * (b + 1))
                if b == 0:
                    pe.wait_ge(dve_const, 6)
                if b >= 2:
                    pe.wait_ge(hT_s, b - 1)
                for j in range(J):
                    t = b * J + j
                    last = pe.matmul(ks_ps[:, 0:NV], k_sb[:, t, :], v_sb[:, t, :], start=j == 0, stop=j == J - 1)
                last.then_inc(ks_mm, 1)

            def product_q(b):
                pe.wait_ge(xnT_s, b + 1)
                if b == 0:
                    pe.wait_ge(wq_in, 16)
                elif b >= 2:
                    pe.wait_ge(x1_s, b - 1)
                else:
                    pe.wait_ge(q_s, b)
                pe.matmul(q_ps[:], wq_sb[:], xnT[:, tiles(b), :].rearrange("p j d -> p (j d)"), start=True, stop=False)
                if b == 0:
                    pe.wait_ge(bias_done, 1)
                pe.matmul(q_ps[:], bias_rows[:, 0:D], ones_bf[:], start=False, stop=True).then_inc(q_mm, 1)

            def product_kv(b):
                if b == 0:
                    pe.wait_ge(wkv_in, 32)
                else:
                    pe.wait_ge(k_s, 2 * b)
                    pe.wait_ge(v_s, 2 * b)
                for j in range(J):
                    dst = kv_ps[:, j, :]
                    pe.matmul(dst, xnT[:, b * J + j, :], wkv_sb[:], start=True, stop=False)
                    last = pe.matmul(dst, ones_bf[:, 0:P], bias_rows[:, D:3 * D], start=False, stop=True)
                    if j % 2:
                        last.then_inc(kv_mm, 1)

            def product_nd(b):
                pe.wait_ge(q_s, b + 1)
                pe.wait_ge(kvd_s, 2 * (b + 1))
                if b >= 1:
                    pe.wait_ge(sc_s, b)
                for j in range(J):
                    last = pe.matmul(nd_ps[:, j, 0:ND], qT[:, b, j * P:(j + 1) * P],
                                     kvd[:, b, :], start=True, stop=True)
                last.then_inc(nd_mm, 1)

            def scores_T(b):
                if b >= 2:
                    pe.wait_ge(rkm_s, b - 1)
                pe.wait_ge(sc_s, b + 1)
                for j in range(J):
                    last = pe.transpose(scT_ps[:, j * P:(j + 1) * P], sc[:, b * J + j, :], ident[:])
                last.then_inc(scT_mm, 1)

            def rows_T(b):
                pe.wait_ge(kvd_s, 2 * min(b + 2, B))
                for j in range(J):
                    pe.wait_ge(h_s, b * J + j + 1)
                    last = pe.transpose(hT_ps[:, j * P:(j + 1) * P], rows[:, b * J + j, 0:D], ident[:])
                last.then_inc(hT_mm, 1)

            def product_o(b):
                pe.wait_ge(scT_s, b + 1)
                pe.wait_ge(q_s, min(b + 2, B))
                if b == 0:
                    pe.wait_ge(wo_in, 16)
                for j in range(J):
                    dst = att_ps[:, j * D:(j + 1) * D]
                    pe.matmul(dst, scT[:, b * J + j, :], wo_sb[:], start=True, stop=False)
                    last = pe.matmul(dst, ones_bf[:, 0:P], bias_rows[:, 3 * D:4 * D], start=False, stop=True)
                last.then_inc(att_mm, 1)

            def logits(b):
                pe.wait_ge(hT_s, b + 1)
                pe.wait_ge(scT_s, min(b + 2, B))
                if b == B - 1:
                    pe.wait_ge(rkm_s, b)
                if b == 0:
                    pe.wait_ge(wr_in, 16)
                for j in range(J):
                    last = pe.matmul(lg_ps[:, j * E:(j + 1) * E], hT[:, b * J + j, :], wr_sb[:], start=True, stop=True)
                last.then_inc(lg_mm, 1)

            def rank_sums(b):
                if b == 0:
                    pe.wait_ge(pool_const, 4)
                pe.wait_ge(onehot_s, b + 1)
                pe.wait_ge(total_s, b + 1)
                t0 = b * J
                rk = rk_ps[:, 0:J * E]
                pe.matmul(rk, before[:], onehot[:, tiles(b), :].rearrange("p j e -> p (j e)"), start=True, stop=False)
                for a in range(b):
                    pe.matmul(rk.rearrange("p (j e) -> p j e", e=E), ones16[:],
                              total[:, a:a + 1, :].broadcast_to([P, J, E]), start=False, stop=False)
                for j in range(J - 1):
                    last = pe.matmul(rk[:, (j + 1) * E:].rearrange("p (j e) -> p j e", e=E), ones16[:],
                                     onehot[:, t0 + j:t0 + j + 1, :].broadcast_to([P, J - 1 - j, E]), start=False,
                                     stop=j == J - 2)
                if b < B - 1:
                    last.then_inc(rk_mm, 1)
                    return
                for a in range(B):
                    last = pe.matmul(cnt_ps[:, CNT:CNT + E], ones16[:], total[:, a, :], start=a == 0, stop=a == B - 1)
                last.then_inc(cnt_mm, 1)

            def keep_warm(n):
                for _ in range(n):
                    pe.matmul(warm_ps[:], ones_bf[:, 0:P], ones_bf[:], start=True, stop=True)

            pe.wait_ge(dve_const, 1)
            keep_warm(WARM_START)
            for s in range(B + 2):
                if s < B:
                    normalised_T(s)
                if 1 <= s <= B:
                    product_ks(s - 1)
                if 3 <= s <= B:
                    rank_sums(s - 3)
                if s < B:
                    product_q(s)
                if 1 <= s <= B:
                    product_nd(s - 1)
                if s >= 2:
                    rows_T(s - 2)
                if s < B:
                    product_kv(s)
                if 1 <= s <= B:
                    scores_T(s - 1)
                if s >= 2:
                    logits(s - 2)
                if 1 <= s <= B:
                    product_o(s - 1)
                if s == B:
                    rank_sums(B - 2)
            pe.wait_ge(b1_in, 16)
            pe.wait_ge(sc_s, B)
            pe.transpose(b1_ps[:, 0:E * FC], b1_rows[:], ident[0:E * FC, 0:E * FC]).then_inc(b1_mm, 1)
            rank_sums(B - 1)
            keep_warm(WARM_ROUTING)

            def slots_T(i, r, k, turn):
                if not (isinstance(i, int) and i < 2):
                    pe.wait_ge(tT_s, i - 1)
                pe.wait_ge(slot_h_in[r], turn * 16)
                pe.transpose(tT_ps[k][:, 0:P], slot_h[:, r, :], ident[:]).then_inc(tT_mm, 1)

            def hidden(i, r, k):
                pe.wait_ge(tT_s, i + 1)
                pe.wait_ge(w1_s, i + 1)
                if not (isinstance(i, int) and i < 2):
                    pe.wait_ge(hid_s, (i - 1) * FC)
                for c in range(FC):
                    last = pe.matmul(hid_ps[k][:, c * P:(c + 1) * P], w1_st[:, k, c * P:(c + 1) * P], tT[:, r, :],
                                     start=True, stop=True)
                last.then_inc(hid_mm, 1)

            def down(i, k):
                pe.wait_ge(hid_s, (i + 1) * FC)
                pe.wait_ge(w2_s, i + 1)
                if not (isinstance(i, int) and i < 2):
                    pe.wait_ge(yb_s, i - 1)
                for c in range(FC):
                    last = pe.matmul(y_ps[k][:, 0:D], hid[:, k, c, :], w2_st[:, k, c, :], start=c == 0, stop=c == FC - 1)
                last.then_inc(y_mm, 1)

            pe.wait_ge(b1_s, 1)
            slots_T(0, 0, 0, 1)
            slots_T(1, 1, 1, 1)
            hidden(0, 0, 0)
            for i in range(2):
                slots_T(i + 2, i + 2, i % 2, 1)
                hidden(i + 1, i + 1, (i + 1) % 2)
                down(i, i % 2)
            loops = (SLOT_TILES - 4) // RING
            with pe.Fori(0, loops) as m:
                for r in range(RING):
                    i = m * RING + r + 2
                    slots_T(i + 2, r, r % 2, m + 2)
                    hidden(i + 1, (r + 3) % RING, (r + 1) % 2)
                    down(i, r % 2)
            for i in range(loops * RING + 2, SLOT_TILES):
                if i + 2 < SLOT_TILES:
                    slots_T(i + 2, (i + 2) % RING, i % 2, (i + 2) // RING + 1)
                if i + 1 < SLOT_TILES:
                    hidden(i + 1, (i + 1) % RING, (i + 1) % 2)
                down(i, i % 2)


_INS = ['L0_attn_x', 'L0_attn_wq', 'L0_attn_bq', 'L0_attn_wk', 'L0_attn_bk', 'L0_attn_wv', 'L0_attn_bv', 'L0_attn_wo',
        'L0_attn_bo', 'L0_ffn_Wr', 'L0_ffn_W1', 'L0_ffn_b1', 'L0_ffn_W2', 'L0_ffn_b2']


def kernel(**inputs):
    import numpy as _np
    import concourse.bacc as _bacc
    from concourse import mybir as _mybir
    from concourse.bass_utils import run_bass_kernel_spmd as _run

    nc = _bacc.Bacc("TRN2", target_bir_lowering=False, num_devices=1)
    arrays, args = {}, []
    for name in _INS:
        a = _np.ascontiguousarray(inputs[name])
        arrays[f"in_{name}_dram"] = a
        args.append(nc.dram_tensor(f"in_{name}_dram", a.shape, _mybir.dt.from_np(a.dtype), kind="ExternalInput").ap())
    shape = inputs['L0_attn_x'].shape
    args.append(nc.dram_tensor("out_0_dram", shape, _mybir.dt.float32, kind="ExternalOutput").ap())
    preln_linear_attention_moe(nc, *args)
    r = _run(nc, [arrays], core_ids=[0])
    return r.results[0]["out_0_dram"]
```

```python
from contextlib import ExitStack

import concourse.bass as bass
from concourse import mybir

F32 = mybir.dt.float32
F16 = mybir.dt.float16
BF16 = mybir.dt.bfloat16
I32 = mybir.dt.int32
U32 = mybir.dt.uint32
ALU = mybir.AluOpType
ACT = mybir.ActivationFunctionType
AX_X = mybir.AxisListType.X

P = 128
HEADS = 16
LN_EPS = 1e-5
DEN_EPS = 1e-6
WARM_START = 14
WARM_ROUTING = 42
WARM_FIRST = 4
WARM_LAST = (3, 6, 10, 1, 3, 5)
VEC = 2


def preln_linear_attention_moe(nc, x, wq, bq, wk, bk, wv, bv, wo, bo, Wr, W1, b1, W2, b2, out):
    B, N, D = x.shape
    E, _, F = W1.shape
    assert D == P and N % P == 0 and F % P == 0
    J = N // P
    T = B * J
    TOK = B * N
    HD = D // HEADS
    FC = F // P
    SLOT_TILES = T + E - 1
    RING = 4
    PROB, NUMBER = D, D + 1
    TAIL = D + 4
    ROW = D + TAIL
    REGION = TOK + P
    NV = D + 1
    ND = D + HEADS
    CNT = J * E
    SKIP = 2 * TOK
    FAR = (E + 1) * REGION

    with ExitStack() as ctx:
        def sb(name, shape, dt=F32):
            return ctx.enter_context(nc.sbuf_tensor(name, shape, dt))

        def ps(name, shape, dt=F32):
            return ctx.enter_context(nc.psum_tensor(name, shape, dt))

        def sem(name):
            return ctx.enter_context(nc.semaphore(name))

        rows_dram = nc.dram_tensor("routed_rows", [(E + 1) * REGION, ROW], F32, kind="Internal").ap()

        x_sb = sb("x_sb", [P, T, D])
        wq_sb = sb("wq_sb", [P, D])
        wkv_sb = sb("wkv_sb", [P, 2 * D])
        wo_sb = sb("wo_sb", [P, D])
        wr_sb = sb("wr_sb", [P, E])
        w1_sb = sb("w1_sb", [P, E, F])
        w2_sb = sb("w2_sb", [P, E, FC, D])
        b1_rows = sb("b1_rows", [E * FC, P])
        b1_sb = sb("b1_sb", [P, E * FC])
        b2_sb = sb("b2_sb", [P, E * D])
        bias_in = sb("bias_in", [P, 4 * D])
        bias_b = sb("bias_b", [P, 4 * D])
        bias_hi = sb("bias_hi", [P, 4 * D], BF16)
        bias_rest = sb("bias_rest", [P, 4 * D])
        bias_mid = sb("bias_mid", [P, 4 * D], BF16)
        part_mask = sb("part_mask", [P, 1])
        part_step = sb("part_step", [P, 2])
        bias_rows = sb("bias_rows", [P, 4 * D], BF16)

        ident = sb("ident", [P, P])
        head_mask = sb("head_mask", [P, D])
        head_sel = sb("head_sel", [P, HEADS])
        before = sb("before", [P, P], F16)
        ones16 = sb("ones16", [P, P], F16)
        ones_bf = sb("ones_bf", [P, N], BF16)
        region = sb("region", [P, J, E])
        region_row = sb("region_row", [1, E])
        tile_row0 = sb("tile_row0", [1, SLOT_TILES])
        tile_thr = sb("tile_thr", [1, E, T])
        tile_no = sb("tile_no", [1, SLOT_TILES, E])
        ones_e = sb("ones_e", [1, E])
        pad_rows = sb("pad_rows", [P, ROW])
        minus_half = sb("minus_half", [P, J])

        st1 = sb("st1", [P, T, 6])
        mv1 = sb("mv1", [P, T, 2])
        ve1 = sb("ve1", [P, T])
        nm1 = sb("nm1", [P, T])
        rs1 = sb("rs1", [P, T])
        nmr1 = sb("nmr1", [P, T])
        xn = sb("xn", [P, T, D])
        xnT = sb("xnT", [P, T, D])
        e_q = sb("e_q", [P, B, N])
        qT = sb("qT", [P, B, N])
        e_k = sb("e_k", [P, T, D])
        k_sb = sb("k_sb", [P, T, D])
        v_sb = sb("v_sb", [P, T, NV])
        kvd = sb("kvd", [P, B, ND])
        den = sb("den", [P, T, HEADS])
        zed = sb("zed", [P, T, HEADS])
        sc = sb("sc", [P, T, D])
        scT = sb("scT", [P, T, D])
        st2 = sb("st2", [P, T, 6])
        mv2 = sb("mv2", [P, T, 2])
        ve2 = sb("ve2", [P, T])
        nm2 = sb("nm2", [P, T])
        rs2 = sb("rs2", [P, T])
        rows = sb("rows", [P, T, ROW])
        hT = sb("hT", [P, T, D])
        lmax = sb("lmax", [P, T])
        lm = sb("lm", [P, T, E])
        pick = sb("pick", [P, T, E])
        first = sb("first", [P, T])
        onehot = sb("onehot", [P, T, E], F16)
        total = sb("total", [P, B, E], F16)
        ex = sb("ex", [P, T, E])
        exsum = sb("exsum", [P, T])
        rk_m = sb("rk_m", [P, T, E])
        rank = sb("rank", [P, T])
        slot = sb("slot", [P, T], I32)
        pad_at = sb("pad_at", [1, E], I32)
        over = sb("over", [1, E, T])
        tiles_e = sb("tiles_e", [1, E])
        tiles_incl = sb("tiles_incl", [1, E])
        past = sb("past", [1, SLOT_TILES, E])
        tile_expert = sb("tile_expert", [1, SLOT_TILES], I32)
        skip_e = sb("skip_e", [1, E - 1])
        skipped = sb("skipped", [1, SLOT_TILES, E - 1])
        skipped_n = sb("skipped_n", [1, SLOT_TILES])
        start_own = sb("start_own", [1, SLOT_TILES])
        bound = sb("bound", [1, SLOT_TILES])
        tile_start = sb("tile_start", [1, SLOT_TILES], I32)

        slot_h = sb("slot_h", [P, RING, D])
        slot_x = sb("slot_x", [P, RING, TAIL])
        tT = sb("tT", [P, RING, P])
        w1_st = sb("w1_st", [P, 2, F])
        w2_st = sb("w2_st", [P, 2, FC, D])
        b1_st = sb("b1_st", [P, 2, FC])
        hid = sb("hid", [P, 2, FC, P])
        yb = sb("yb", [P, RING, D])
        y_sb = sb("y_sb", [P, RING, D])

        pair23 = ps("bank23", [P, 2, 512])
        pair56 = ps("bank56", [P, 2, 512])
        bank = {i: ps(f"bank{i}", [P, 512]) for i in (0, 1, 4, 7)}
        bank |= {2: pair23[:, 0], 3: pair23[:, 1], 5: pair56[:, 0], 6: pair56[:, 1]}
        xnT_ps = bank[0]
        att_ps = bank[1]
        q_ps = bank[1]
        kv_ps = pair23[:].rearrange("p a (j c) -> p (a j) c", j=2)
        ks_ps = bank[4]
        hT_ps = bank[4]
        nd_ps = pair56[:].rearrange("p a (j c) -> p (a j) c", j=2)
        scT_ps = bank[7]
        lg_ps = bank[7][:, 0:J * E]
        rk_ps = bank[0][:, 0:J * E]
        b1_ps = bank[5]
        cnt_ps = bank[0]
        warm_ps = bank[2]
        tT_ps = [bank[0], bank[4]]
        hid_ps = [bank[2], bank[3]]
        y_ps = [bank[5], bank[6]]

        x_in = [sem(f"x_in{b}") for b in range(B)]
        wq_in, wkv_in, bias_in_s, wo_in, wr_in = sem("wq_in"), sem("wkv_in"), sem("bias_in_s"), sem("wo_in"), sem("wr_in")
        b1_in, b2_in, w1_in, w2_in = sem("b1_in"), sem("b2_in"), sem("w1_in"), sem("w2_in")
        pool_set, pool_const = sem("pool_set"), sem("pool_const")
        masks_s, xnv_s, dve_const, bias_ch, bias_done = sem("masks_s"), sem("xnv_s"), sem("dve_const"), sem("bias_ch"), sem("bias_done")
        st1_s, mv1_s, ve1_s, rs1_s, nmr1_s, xn_s = sem("st1_s"), sem("mv1_s"), sem("ve1_s"), sem("rs1_s"), sem("nmr1_s"), sem("xn_s")
        xnT_mm, xnT_s = sem("xnT_mm"), sem("xnT_s")
        q_mm, eq_s, q_s = sem("q_mm"), sem("eq_s"), sem("q_s")
        kv_mm, ek_s, k_s, v_s = sem("kv_mm"), sem("ek_s"), sem("k_s"), sem("v_s")
        ks_mm, kvd_s = sem("ks_mm"), sem("kvd_s")
        nd_mm, den_s, zed_s, sc_s = sem("nd_mm"), sem("den_s"), sem("zed_s"), sem("sc_s")
        scT_mm, scT_s = sem("scT_mm"), sem("scT_s")
        att_mm, x1_s = sem("att_mm"), sem("x1_s")
        st2_s, mv2_s, ve2_s, rs2_s, h_s = sem("st2_s"), sem("mv2_s"), sem("ve2_s"), sem("rs2_s"), sem("h_s")
        hT_mm, hT_s = sem("hT_mm"), sem("hT_s")
        lg_mm, lmax_s, lm_s, pick_s, first_s, onehot_s, total_s = (sem("lg_mm"), sem("lmax_s"), sem("lm_s"), sem("pick_s"),
                                                                  sem("first_s"), sem("onehot_s"), sem("total_s"))
        ex_s, exsum_s, prob_s = sem("ex_s"), sem("exsum_s"), sem("prob_s")
        rk_mm, rkm_s, rank_s, slot_s, number_s = sem("rk_mm"), sem("rkm_s"), sem("rank_s"), sem("slot_s"), sem("number_s")
        rows_out, pads_out = sem("rows_out"), sem("pads_out")
        cnt_mm, route_ch, pad_at_s, tile_expert_s, tile_start_s = (sem("cnt_mm"), sem("route_ch"), sem("pad_at_s"),
                                                                   sem("tile_expert_s"), sem("tile_start_s"))
        b1_mm, b1_s = sem("b1_mm"), sem("b1_s")
        slot_h_in = [sem(f"slot_h_in{r}") for r in range(RING)]
        slot_x_in = [sem(f"slot_x_in{r}") for r in range(RING)]
        y_out = [sem(f"y_out{r}") for r in range(RING)]
        tT_mm, tT_s, w1_s, b1st_s, w2_s = sem("tT_mm"), sem("tT_s"), sem("w1_s"), sem("b1st_s"), sem("w2_s")
        hid_mm, hid_s, y_mm, yb_s, y_s = sem("hid_mm"), sem("hid_s"), sem("y_mm"), sem("yb_s"), sem("y_s")

        block = ctx.enter_context(nc.Block())

        x_v = x.rearrange("b (p j) d -> b p j d", j=J)
        out_flat = out.rearrange("b n d -> (b n) d")

        def tiles(b):
            return slice(b * J, (b + 1) * J)

        def tile_values(engine, table, i, n, top):
            cols = table[0:1, i:i + n] if isinstance(i, int) else table[0:1, bass.ds(i, n)]
            return nc.values_load_multi_w_load_instructions(
                cols, engines=[engine], min_val=0, max_val=top,
                skip_runtime_bounds_check_because="sums of counts of tokens and tiles, which the shapes bound")[1]

        def pad_experts(eng, engine, experts):
            eng.wait_ge(number_s, 2)
            eng.wait_ge(pad_at_s, 1)
            for at in tile_values(engine, pad_at, experts[0], len(experts), (E + 1) * REGION - P):
                eng.dma_start(rows_dram[bass.ds(at, P), :], pad_rows[:]).then_inc(pads_out, 16)

        @block.sync
        def _(sp):
            sp.dma_start(x_sb[:, tiles(0), :], x_v[0]).then_inc(x_in[0], 16)
            sp.dma_start(x_sb[:, tiles(1), :], x_v[1]).then_inc(x_in[1], 16)
            for i, bias in enumerate((bq, bk, bv, bo)):
                sp.dma_start(bias_in[:, i * D:(i + 1) * D], bias.partition_broadcast(P)).then_inc(bias_in_s, 16)
            for b in range(2, B):
                sp.dma_start(x_sb[:, tiles(b), :], x_v[b]).then_inc(x_in[b], 16)
            sp.dma_start(wo_sb[:], wo).then_inc(wo_in, 16)
            sp.dma_start(wr_sb[:], Wr).then_inc(wr_in, 16)
            sp.dma_start(b1_rows[:], b1.rearrange("e (c p) -> (e c) p", p=P)).then_inc(b1_in, 16)
            for h in range(2):
                es = slice(h * E // 2, (h + 1) * E // 2)
                sp.dma_start(w1_sb[:, es, :], W1[es].rearrange("e d f -> d e f")).then_inc(w1_in, 16)
            for e in range(E):
                sp.dma_start(w2_sb[:, e], W2[e].rearrange("(c p) d -> p c d", p=P)).then_inc(w2_in, 16)
            sp.dma_start(b2_sb[:], b2.rearrange("e d -> (e d)").partition_broadcast(P)).then_inc(b2_in, 16)

            pad_experts(sp, mybir.EngineType.SP, range(E // 2))

            def first_rows(i, n):
                return tile_values(mybir.EngineType.SP, tile_start, i, n, (E + 1) * REGION - P)

            def load_h(at, r, transposed):
                if transposed is not None:
                    sp.wait_ge(tT_mm, transposed)
                sp.dma_start(slot_h[:, r, :], rows_dram[bass.ds(at, P), 0:D]).then_inc(slot_h_in[r], 16)

            def load_x(at, r, old):
                if old is not None:
                    sp.wait_ge(y_out[r], old)
                sp.dma_start(slot_x[:, r, :], rows_dram[bass.ds(at, P), D:ROW]).then_inc(slot_x_in[r], 16)

            sp.wait_ge(tile_start_s, 1)
            sp.wait_ge(rows_out, 16 * T)
            sp.wait_ge(pads_out, 16 * E)
            at = first_rows(0, RING)
            for i in range(RING):
                load_h(at[i], i, None)
            load_x(at[0], 0, None)
            ahead = first_rows(RING, RING - 1)
            for i in range(RING - 1):
                load_h(ahead[i], i, i + 1)
                load_x(at[i + 1], i + 1, None)
            loops = (SLOT_TILES - 2 * RING + 1) // RING
            with sp.Fori(0, loops) as m:
                at = first_rows(m * RING + RING, RING + 3)
                for r in range(RING):
                    load_h(at[r + 3], (r + 3) % RING, m * RING + r + RING)
                    load_x(at[r], r, m * 16 + 16)
            done = (loops + 1) * RING
            at = first_rows(done, SLOT_TILES - done)
            for i in range(done, SLOT_TILES):
                if i + 3 < SLOT_TILES:
                    load_h(at[i + 3 - done], (i + 3) % RING, i + 4 - RING)
                load_x(at[i - done], i % RING, i // RING * 16)
            for r in range(RING):
                sp.wait_ge(y_out[r], 16 * ((SLOT_TILES - r + RING - 1) // RING))

        @block.gpsimd
        def _(pool):
            n = [0]

            def cleared(ins):
                n[0] += 1
                ins.then_inc(pool_set, 1)
                pool.wait_ge(pool_set, n[0])

            def select(t, pattern, cm, op, fill, base=0):
                return pool.affine_select(out=t, in_=t, compare_op=op, fill=fill, base=base, pattern=pattern,
                                          channel_multiplier=cm)

            cleared(pool.memset(ident[:], 0.0))
            select(ident[:], [[-1, P]], 1, ALU.not_equal, 1.0).then_inc(pool_const, 1)
            pool.memset(minus_half[:], -0.5).then_inc(pool_const, 1)
            cleared(pool.memset(part_mask[:], 1.0))
            select(part_mask[:], [[0, 1]], -1, ALU.is_ge, 0.0, base=2).then_inc(masks_s, 1)
            cleared(pool.memset(part_step[:], -1.0))
            select(part_step[:], [[-1, 2]], 1, ALU.is_ge, 0.0, base=-1).then_inc(masks_s, 1)

            def ln_scale(b, mv_s, mv, ve_s, ve, nm, rs_s, rs):
                pool.wait_ge(mv_s, J * (b + 1))
                pool.tensor_scalar(ve[:, tiles(b)], mv[:, tiles(b), 1], LN_EPS, None, ALU.add).then_inc(ve_s, 1)
                pool.tensor_scalar(nm[:, tiles(b)], mv[:, tiles(b), 0], -1.0, None, ALU.mult).then_inc(ve_s, 1)
                pool.wait_ge(ve_s, 2 * (b + 1))
                pool.tensor_tensor(rs[:, tiles(b)], ve[:, tiles(b)], minus_half[:], ALU.pow).then_inc(rs_s, 1)
                pool.wait_ge(rs_s, b + 1)

            def ln1(b):
                ln_scale(b, mv1_s, mv1, ve1_s, ve1, nm1, rs1_s, rs1)
                pool.tensor_tensor(nmr1[:, tiles(b)], nm1[:, tiles(b)], rs1[:, tiles(b)], ALU.mult).then_inc(nmr1_s, 1)

            def ln2(b):
                if b == B - 1:
                    pool.wait_ge(ve2_s, 2 * (b + 1))
                    pool.tensor_tensor(rs2[:, tiles(b)], ve2[:, tiles(b)], minus_half[:], ALU.pow).then_inc(rs2_s, 1)
                    return
                ln_scale(b, mv2_s, mv2, ve2_s, ve2, nm2, rs2_s, rs2)
                for t in range(b * J, (b + 1) * J):
                    pool.tensor_scalar(rows[:, t, 0:D], rows[:, t, D:2 * D], nm2[:, t:t + 1], rs2[:, t:t + 1],
                                       ALU.add, ALU.mult).then_inc(h_s, 1)

            def scatter_rows(b):
                pool.wait_ge(slot_s, b + 1)
                pool.wait_ge(prob_s, b + 1)
                pool.wait_ge(h_s, J * (b + 1))
                for t in range(b * J, (b + 1) * J):
                    pool.indirect_dma_start(
                        out=rows_dram, out_offset=bass.IndirectOffsetOnAxis(ap=slot[:, t:t + 1].bitcast(U32), axis=0),
                        in_=rows[:, t, :], in_offset=None, bounds_check=(E + 1) * REGION - 1, oob_is_err=False)\
                        .then_inc(rows_out, 16)

            def scatter_output(i):
                r = i % RING
                pool.wait_ge(y_s, i + 1)
                pool.indirect_dma_start(
                    out=out_flat,
                    out_offset=bass.IndirectOffsetOnAxis(ap=slot_x[:, r, NUMBER:NUMBER + 1].bitcast(U32), axis=0),
                    in_=y_sb[:, r, :], in_offset=None, bounds_check=TOK - 1, oob_is_err=False)\
                    .then_inc(y_out[r], 16)

            ln1(0)
            cleared(pool.memset(head_mask[:], 1.0))
            hm = head_mask[:].rearrange("p (h e) -> p h e", e=HD)
            cleared(select(hm, [[-HD, HEADS], [0, HD]], 1, ALU.is_ge, 0.0))
            cleared(select(hm, [[HD, HEADS], [0, HD]], -1, ALU.is_ge, 0.0, base=HD - 1))
            cleared(pool.memset(head_sel[:], 1.0))
            cleared(select(head_sel[:], [[-HD, HEADS]], 1, ALU.is_ge, 0.0))
            select(head_sel[:], [[HD, HEADS]], -1, ALU.is_ge, 0.0, base=HD - 1).then_inc(pool_const, 1)
            ln1(1)
            cleared(pool.memset(before[:], 1.0))
            select(before[:], [[1, P]], -1, ALU.is_gt, 0.0).then_inc(pool_const, 1)
            pool.iota(region[:], pattern=[[0, J], [-1, E]], base=E, channel_multiplier=0,
                      allow_small_or_imprecise_dtypes=True).then_inc(pool_const, 1)
            ln1(2)
            ln1(3)
            pool.wait_ge(dve_const, 6)
            pool.iota(rows[:, :, D + NUMBER].bitcast(I32), pattern=[[N, B], [1, J]], base=0, channel_multiplier=J)\
                .then_inc(number_s, 1)
            pool.iota(pad_rows[:, D + NUMBER:D + NUMBER + 1].bitcast(I32), pattern=[[0, 1]], base=SKIP,
                      channel_multiplier=0).then_inc(number_s, 1)
            pool.iota(region_row[:], pattern=[[-REGION, E]], base=E * REGION, channel_multiplier=0,
                      allow_small_or_imprecise_dtypes=True).then_inc(pool_const, 1)
            pool.iota(tile_row0[:], pattern=[[P, SLOT_TILES]], base=E * REGION, channel_multiplier=0,
                      allow_small_or_imprecise_dtypes=True).then_inc(pool_const, 1)
            pool.iota(tile_thr[:], pattern=[[0, E], [P, T]], base=0, channel_multiplier=0,
                      allow_small_or_imprecise_dtypes=True).then_inc(pool_const, 1)
            pool.iota(tile_no[:], pattern=[[1, SLOT_TILES], [0, E]], base=0, channel_multiplier=0,
                      allow_small_or_imprecise_dtypes=True).then_inc(pool_const, 1)
            pool.wait_ge(number_s, 1)
            ln2(0)
            ln2(1)
            scatter_rows(0)
            ln2(2)
            scatter_rows(1)
            ln2(3)
            scatter_rows(2)
            scatter_rows(3)
            for i in range(SLOT_TILES):
                scatter_output(i)

        @block.scalar
        def _(act):
            act.dma_start(wq_sb[:], wq).then_inc(wq_in, 16)
            act.dma_start(wkv_sb[:, 0:D], wk).then_inc(wkv_in, 16)
            act.dma_start(wkv_sb[:, D:2 * D], wv).then_inc(wkv_in, 16)
            act.preload_act_table(ACT.Exp)

            def normalise(b):
                act.wait_ge(x_in[b], 16)
                act.wait_ge(nmr1_s, b + 1)
                for t in range(b * J, (b + 1) * J - (VEC if b == 0 else 0)):
                    act.activation(xn[:, t, :], x_sb[:, t, :], ACT.Identity, bias=nmr1[:, t:t + 1],
                                   scale=rs1[:, t:t + 1]).then_inc(xn_s, 1)

            def copy_xnT(b):
                act.wait_ge(xnT_mm, b + 1)
                act.copy(xnT[:, tiles(b), :], xnT_ps[:].rearrange("p (j d) -> p j d", j=J)).then_inc(xnT_s, 1)

            def exp_q(b):
                act.wait_ge(q_mm, b + 1)
                act.activation(e_q[:, b, :], q_ps[:], ACT.Exp, bias=-1.0).then_inc(eq_s, 1)

            def exp_k_copy_v(b):
                for h in range(2):
                    act.wait_ge(kv_mm, 2 * b + h + 1)
                    ts = slice(b * J + 2 * h, b * J + 2 * h + 2)
                    kv = kv_ps[:, 2 * h:2 * h + 2, :]
                    act.activation(e_k[:, ts, :], kv[:, :, 0:D], ACT.Exp, bias=-1.0).then_inc(ek_s, 1)
                    act.copy(v_sb[:, ts, 0:D], kv[:, :, D:2 * D]).then_inc(v_s, 1)

            def copy_scT(b):
                act.wait_ge(scT_mm, b + 1)
                act.copy(scT[:, tiles(b), :], scT_ps[:].rearrange("p (j d) -> p j d", j=J)).then_inc(scT_s, 1)

            def copy_hT(b):
                act.wait_ge(hT_mm, b + 1)
                act.copy(hT[:, tiles(b), :], hT_ps[:].rearrange("p (j d) -> p j d", j=J)).then_inc(hT_s, 1)

            def exp_logits(b):
                act.wait_ge(lm_s, b + 1)
                act.activation(ex[:, tiles(b), :], lm[:, tiles(b), :], ACT.Exp).then_inc(ex_s, 1)

            normalise(0)
            for s in range(B + 2):
                if s < B:
                    copy_xnT(s)
                    if s + 1 < B:
                        normalise(s + 1)
                if 3 <= s <= B:
                    exp_logits(s - 3)
                if s < B:
                    exp_q(s)
                    exp_k_copy_v(s)
                if 1 <= s <= B:
                    copy_scT(s - 1)
                if s >= 2:
                    copy_hT(s - 2)
                if s == B:
                    exp_logits(s - 2)
            exp_logits(B - 1)
            act.wait_ge(b1_mm, 1)
            act.copy(b1_sb[:], b1_ps[:, 0:E * FC]).then_inc(b1_s, 1)
            act.preload_act_table(ACT.Gelu)
            pad_experts(act, mybir.EngineType.Activation, range(E // 2, E))

            def copy_tT(i, r, k):
                act.wait_ge(tT_mm, i + 1)
                act.copy(tT[:, r, :], tT_ps[k][:, 0:P]).then_inc(tT_s, 1)

            def gelu(i, k):
                act.wait_ge(hid_mm, i + 1)
                act.wait_ge(b1st_s, i + 1)
                for c in range(FC):
                    act.activation(hid[:, k, c, :], hid_ps[k][:, c * P:(c + 1) * P], ACT.Gelu,
                                   bias=b1_st[:, k, c:c + 1]).then_inc(hid_s, 1)

            copy_tT(0, 0, 0)
            copy_tT(1, 1, 1)
            gelu(0, 0)
            loops = (SLOT_TILES - 2) // RING
            with act.Fori(0, loops) as m:
                for r in range(RING):
                    i = m * RING + r
                    copy_tT(i + 2, (r + 2) % RING, r % 2)
                    gelu(i + 1, (r + 1) % 2)
            for i in range(loops * RING, SLOT_TILES):
                if i + 2 < SLOT_TILES:
                    copy_tT(i + 2, (i + 2) % RING, i % 2)
                if i + 1 < SLOT_TILES:
                    gelu(i + 1, (i + 1) % 2)

        @block.vector
        def _(dve):
            dve.memset(ones_bf[:], 1.0).then_inc(dve_const, 1)
            dve.memset(ones16[:], 1.0).then_inc(dve_const, 1)
            dve.memset(ones_e[:], 1.0).then_inc(dve_const, 1)
            dve.memset(v_sb[:, :, D:NV], 1.0).then_inc(dve_const, 1)
            dve.memset(rows[:, :, 2 * D:ROW], 0.0).then_inc(dve_const, 1)
            dve.memset(pad_rows[:], 0.0).then_inc(dve_const, 1)

            def moments(t0, src, st_s, st, mv_s, mv):
                for t in range(t0, t0 + J):
                    dve.bn_stats(st[:, t, :], src[:, t, :]).then_inc(st_s, 1)
                for t in range(t0, t0 + J):
                    dve.wait_ge(st_s, t + 1)
                    dve.bn_aggr(mv[:, t, :], st[:, t, :]).then_inc(mv_s, 1)

            def moments1(b):
                dve.wait_ge(x_in[b], 16)
                moments(b * J, x_sb, st1_s, st1, mv1_s, mv1)

            def bias_parts():
                c = [0]

                def step(ins):
                    c[0] += 1
                    ins.then_inc(bias_ch, 1)
                    dve.wait_ge(bias_ch, c[0])
                dve.wait_ge(bias_in_s, 64)
                dve.wait_ge(masks_s, 2)
                dve.tensor_scalar(bias_b[:, 2 * D:], bias_in[:, 2 * D:], part_mask[:], None, ALU.mult)\
                    .then_inc(bias_ch, 1)
                c[0] += 1
                step(dve.tensor_scalar(bias_b[:, 0:2 * D], bias_in[:, 0:2 * D], 1.0, part_mask[:], ALU.add, ALU.mult))
                step(dve.tensor_copy(bias_hi[:], bias_b[:]))
                step(dve.scalar_tensor_tensor(out=bias_rest[:], in0=bias_hi[:], scalar=part_step[:, 0:1],
                                              in1=bias_b[:], op0=ALU.mult, op1=ALU.add))
                step(dve.tensor_copy(bias_mid[:], bias_rest[:]))
                dve.scalar_tensor_tensor(out=bias_rows[:], in0=bias_mid[:], scalar=part_step[:, 1:2],
                                         in1=bias_rest[:], op0=ALU.mult, op1=ALU.add).then_inc(bias_done, 1)

            def feature_q(b):
                dve.wait_ge(eq_s, b + 1)
                dve.scalar_tensor_tensor(out=qT[:, b, :], in0=e_q[:, b, :], scalar=1.0, in1=q_ps[:], op0=ALU.min,
                                         op1=ALU.max).then_inc(q_s, 1)

            def feature_k(b):
                for h in range(2):
                    ts = slice(b * J + 2 * h, b * J + 2 * h + 2)
                    kv = kv_ps[:, 2 * h:2 * h + 2, :]
                    dve.wait_ge(v_s, 2 * b + h + 1)
                    dve.scalar_tensor_tensor(out=k_sb[:, ts, :], in0=e_k[:, ts, :], scalar=1.0, in1=kv[:, :, 0:D],
                                             op0=ALU.min, op1=ALU.max).then_inc(k_s, 1)

            def head_blocks(b):
                dve.wait_ge(ks_mm, b + 1)
                if b == 0:
                    dve.wait_ge(pool_const, 3)
                dve.tensor_tensor(kvd[:, b, 0:D], ks_ps[:, 0:D], head_mask[:], ALU.mult).then_inc(kvd_s, 1)
                dve.tensor_scalar(kvd[:, b, D:ND], head_sel[:], ks_ps[:, D:NV], None, ALU.mult).then_inc(kvd_s, 1)

            def attend(b):
                dve.wait_ge(nd_mm, b + 1)
                dve.tensor_scalar(den[:, tiles(b), :], nd_ps[:, :, D:ND], DEN_EPS, None, ALU.add).then_inc(den_s, 1)
                dve.wait_ge(den_s, b + 1)
                dve.reciprocal(zed[:, tiles(b), :], den[:, tiles(b), :]).then_inc(zed_s, 1)
                dve.wait_ge(zed_s, b + 1)
                dve.tensor_tensor(sc[:, tiles(b), :].rearrange("p j (h e) -> p j h e", e=HD),
                                  nd_ps[:, :, 0:D].rearrange("p j (h e) -> p j h e", e=HD),
                                  zed[:, tiles(b), :].unsqueeze(3).broadcast_to([P, J, HEADS, HD]), ALU.mult)\
                    .then_inc(sc_s, 1)

            def residual(b):
                dve.wait_ge(att_mm, b + 1)
                dve.tensor_tensor(rows[:, tiles(b), D:2 * D], att_ps[:].rearrange("p (j d) -> p j d", j=J),
                                  x_sb[:, tiles(b), :], ALU.add).then_inc(x1_s, 1)
                dve.wait_ge(x1_s, b + 1)
                moments(b * J, rows[:, :, D:2 * D], st2_s, st2, mv2_s, mv2)

            def last_scales(b):
                dve.wait_ge(mv2_s, J * (b + 1))
                dve.tensor_scalar(ve2[:, tiles(b)], mv2[:, tiles(b), 1], LN_EPS, None, ALU.add).then_inc(ve2_s, 1)
                dve.tensor_scalar(nm2[:, tiles(b)], mv2[:, tiles(b), 0], -1.0, None, ALU.mult).then_inc(ve2_s, 1)

            def last_rows(b):
                dve.wait_ge(ve2_s, 2 * (b + 1))
                dve.wait_ge(rs2_s, b + 1)
                for t in range(b * J, (b + 1) * J):
                    dve.tensor_scalar(rows[:, t, 0:D], rows[:, t, D:2 * D], nm2[:, t:t + 1], rs2[:, t:t + 1],
                                      ALU.add, ALU.mult).then_inc(h_s, 1)

            def route(b):
                ts = tiles(b)
                lg = lg_ps.rearrange("p (j e) -> p j e", j=J)
                dve.wait_ge(lg_mm, b + 1)
                dve.tensor_reduce(lmax[:, ts], lg, AX_X, ALU.max).then_inc(lmax_s, 1)
                dve.wait_ge(lmax_s, b + 1)
                dve.tensor_tensor(lm[:, ts, :], lg, lmax[:, ts].unsqueeze(2).broadcast_to([P, J, E]), ALU.subtract)\
                    .then_inc(lm_s, 1)
                dve.wait_ge(lm_s, b + 1)
                if b == 0:
                    dve.wait_ge(pool_const, 5)
                dve.scalar_tensor_tensor(out=pick[:, ts, :], in0=lm[:, ts, :], scalar=0.0, in1=region[:],
                                         op0=ALU.is_equal, op1=ALU.mult).then_inc(pick_s, 1)
                dve.wait_ge(pick_s, b + 1)
                dve.tensor_reduce(first[:, ts], pick[:, ts, :], AX_X, ALU.max).then_inc(first_s, 1)
                dve.wait_ge(first_s, b + 1)
                dve.tensor_tensor(onehot[:, ts, :], region[:], first[:, ts].unsqueeze(2).broadcast_to([P, J, E]),
                                  ALU.is_equal).then_inc(onehot_s, 1)
                dve.wait_ge(onehot_s, b + 1)
                with nc.allow_low_precision(reason="counts up to the tiles of a batch"):
                    dve.tensor_reduce(total[:, b, :], onehot[:, ts, :].rearrange("p j e -> p e j"), AX_X, ALU.add)\
                        .then_inc(total_s, 1)

            def top_probability(b):
                dve.wait_ge(ex_s, b + 1)
                dve.tensor_reduce(exsum[:, tiles(b)], ex[:, tiles(b), :], AX_X, ALU.add).then_inc(exsum_s, 1)
                dve.wait_ge(exsum_s, b + 1)
                dve.reciprocal(rows[:, tiles(b), 2 * D], exsum[:, tiles(b)]).then_inc(prob_s, 1)

            def slots(b):
                ts = tiles(b)
                if b < B - 1:
                    dve.wait_ge(rk_mm, b + 1)
                dve.tensor_tensor(rk_m[:, ts, :], rk_ps.rearrange("p (j e) -> p j e", j=J),
                                  onehot[:, ts, :], ALU.mult).then_inc(rkm_s, 1)
                dve.wait_ge(rkm_s, b + 1)
                dve.tensor_reduce(rank[:, ts], rk_m[:, ts, :], AX_X, ALU.add).then_inc(rank_s, 1)
                dve.wait_ge(rank_s, b + 1)
                dve.scalar_tensor_tensor(out=slot[:, ts], in0=first[:, ts], scalar=float(REGION), in1=rank[:, ts],
                                         op0=ALU.mult, op1=ALU.add).then_inc(slot_s, 1)

            moments1(0)
            moments1(1)
            dve.wait_ge(nmr1_s, 1)
            for t in range(J - VEC, J):
                dve.tensor_scalar(xn[:, t, :], x_sb[:, t, :], rs1[:, t:t + 1], nmr1[:, t:t + 1], ALU.mult, ALU.add)\
                    .then_inc(xnv_s, 1)
            bias_parts()
            for b in range(2, B):
                moments1(b)
            for s in range(B + 2):
                if 1 <= s <= B:
                    head_blocks(s - 1)
                if 3 <= s <= B:
                    route(s - 3)
                if s < B:
                    feature_q(s)
                if 1 <= s <= B:
                    attend(s - 1)
                if s < B:
                    feature_k(s)
                if 3 <= s <= B:
                    top_probability(s - 3)
                    slots(s - 3)
                if 1 <= s <= B:
                    residual(s - 1)
                if s == B:
                    last_scales(B - 1)
                if s >= B:
                    route(s - 2)
                if s == B:
                    last_rows(B - 1)
                    top_probability(B - 2)
                    slots(B - 2)
            top_probability(B - 1)

            c = [0]

            def step(ins):
                c[0] += 1
                ins.then_inc(route_ch, 1)
                dve.wait_ge(route_ch, c[0])

            dve.wait_ge(pool_const, 9)
            dve.wait_ge(cnt_mm, 1)
            cnt = cnt_ps[0:1, CNT:CNT + E]
            dve.tensor_tensor(pad_at[:], cnt, region_row[:], ALU.add).then_inc(pad_at_s, 1)
            slots(B - 1)
            step(dve.tensor_tensor(over[:], cnt.unsqueeze(2).broadcast_to([1, E, T]), tile_thr[:], ALU.is_gt))
            step(dve.tensor_reduce(tiles_e[:], over[:], AX_X, ALU.add))
            step(dve.tensor_tensor_scan(tiles_incl[:], ones_e[:], tiles_e[:], 0.0, ALU.mult, ALU.add))
            step(dve.tensor_tensor(past[:], tile_no[:],
                                   tiles_incl[:].unsqueeze(1).broadcast_to([1, SLOT_TILES, E]), ALU.is_ge))
            with nc.allow_low_precision(reason="whole numbers up to the number of experts"):
                dve.tensor_reduce(tile_expert[:], past[:, :, 0:E - 1], AX_X, ALU.add).then_inc(tile_expert_s, 1)
            step(dve.tensor_scalar(skip_e[:], tiles_e[:, 0:E - 1], float(-P), float(-REGION), ALU.mult, ALU.add))
            step(dve.tensor_tensor(skipped[:], past[:, :, 0:E - 1],
                                   skip_e[:].unsqueeze(1).broadcast_to([1, SLOT_TILES, E - 1]), ALU.mult))
            step(dve.tensor_reduce(skipped_n[:], skipped[:], AX_X, ALU.add))
            step(dve.tensor_tensor(start_own[:], skipped_n[:], tile_row0[:], ALU.add))
            step(dve.tensor_scalar(bound[:], past[:, :, E - 2], float(-FAR), cnt_ps[0:1, CNT + E - 1:CNT + E],
                                   ALU.mult, ALU.add))
            dve.scalar_tensor_tensor(out=tile_start[:], in0=bound[:], scalar=float(FAR + REGION), in1=start_own[:],
                                     op0=ALU.add, op1=ALU.min).then_inc(tile_start_s, 1)

            def experts_of(i, n):
                return tile_values(mybir.EngineType.DVE, tile_expert, i, n, E - 1)

            def stage_w1(e, k, old):
                if old is not None:
                    dve.wait_ge(hid_mm, old + 1)
                dve.tensor_copy(w1_st[:, k, :], w1_sb[:].rearrange("p e f -> p (e f)")[:, bass.ds(e * F, F)])\
                    .then_inc(w1_s, 1)

            def stage_w2(e, k, old):
                if old is not None:
                    dve.wait_ge(y_mm, old + 1)
                dve.tensor_copy(b1_st[:, k, :], b1_sb[:, bass.ds(e * FC, FC)]).then_inc(b1st_s, 1)
                dve.tensor_copy(w2_st[:, k].rearrange("p c d -> p (c d)"),
                                w2_sb[:].rearrange("p e c d -> p (e c d)")[:, bass.ds(e * F, F)]).then_inc(w2_s, 1)

            def output_rows(i, e, r, k, old):
                dve.wait_ge(y_mm, i + 1)
                if old is not None:
                    dve.wait_ge(y_out[r], old)
                dve.tensor_tensor(yb[:, r, :], y_ps[k][:, 0:D], b2_sb[:, bass.ds(e * D, D)], ALU.add).then_inc(yb_s, 1)
                dve.wait_ge(yb_s, i + 1)
                dve.scalar_tensor_tensor(out=y_sb[:, r, :], in0=yb[:, r, :], scalar=slot_x[:, r, PROB:PROB + 1],
                                         in1=slot_x[:, r, 0:D], op0=ALU.mult, op1=ALU.add).then_inc(y_s, 1)

            dve.wait_ge(tile_expert_s, 1)
            dve.wait_ge(w1_in, 32)
            dve.wait_ge(b1_s, 1)
            es = experts_of(0, RING + 3)
            for i in range(2):
                stage_w1(es[i], i, None)
            dve.wait_ge(w2_in, 16 * E)
            dve.wait_ge(b2_in, 16)
            for i in range(2):
                stage_w2(es[i], i, None)
            stage_w1(es[2], 0, 0)
            for i in range(RING):
                dve.wait_ge(slot_x_in[i], 16)
                output_rows(i, es[i], i, i % 2, None)
                stage_w2(es[i + 2], i % 2, i)
                stage_w1(es[i + 3], (i + 1) % 2, i + 1)
            loops = (SLOT_TILES - 3) // RING
            with dve.Fori(1, loops) as m:
                es = experts_of(m * RING, RING + 3)
                for r in range(RING):
                    i = m * RING + r
                    dve.wait_ge(slot_x_in[r], (m + 1) * 16)
                    output_rows(i, es[r], r, r % 2, m * 16)
                    stage_w2(es[r + 2], r % 2, i)
                    stage_w1(es[r + 3], (r + 1) % 2, i + 1)
            done = loops * RING
            es = experts_of(done, SLOT_TILES - done)
            for i in range(done, SLOT_TILES):
                dve.wait_ge(slot_x_in[i % RING], (i // RING + 1) * 16)
                output_rows(i, es[i - done], i % RING, i % 2, i // RING * 16)
                if i + 2 < SLOT_TILES:
                    stage_w2(es[i + 2 - done], i % 2, i)
                if i + 3 < SLOT_TILES:
                    stage_w1(es[i + 3 - done], (i + 1) % 2, i + 1)

        @block.tensor
        def _(pe):
            def normalised_T(b):
                if b == 0:
                    pe.wait_ge(pool_const, 1)
                else:
                    pe.wait_ge(xnT_s, b)
                for j in range(J):
                    if b:
                        pe.wait_ge(xn_s, b * J + j + 1 - VEC)
                    elif j < J - VEC:
                        pe.wait_ge(xn_s, j + 1)
                    else:
                        pe.wait_ge(xnv_s, j + 1 - (J - VEC))
                    last = pe.transpose(xnT_ps[:, j * P:(j + 1) * P], xn[:, b * J + j, :], ident[:])
                last.then_inc(xnT_mm, 1)

            def product_ks(b):
                pe.wait_ge(k_s, 2 * (b + 1))
                pe.wait_ge(v_s, 2 * (b + 1))
                if b == 0:
                    pe.wait_ge(dve_const, 6)
                if b >= 2:
                    pe.wait_ge(hT_s, b - 1)
                for j in range(J):
                    t = b * J + j
                    last = pe.matmul(ks_ps[:, 0:NV], k_sb[:, t, :], v_sb[:, t, :], start=j == 0, stop=j == J - 1)
                last.then_inc(ks_mm, 1)

            def product_q(b):
                pe.wait_ge(xnT_s, b + 1)
                if b == 0:
                    pe.wait_ge(wq_in, 16)
                elif b >= 2:
                    pe.wait_ge(x1_s, b - 1)
                else:
                    pe.wait_ge(q_s, b)
                pe.matmul(q_ps[:], wq_sb[:], xnT[:, tiles(b), :].rearrange("p j d -> p (j d)"), start=True, stop=False)
                if b == 0:
                    pe.wait_ge(bias_done, 1)
                pe.matmul(q_ps[:], bias_rows[:, 0:D], ones_bf[:], start=False, stop=True).then_inc(q_mm, 1)

            def product_kv(b):
                if b == 0:
                    pe.wait_ge(wkv_in, 32)
                else:
                    pe.wait_ge(k_s, 2 * b)
                    pe.wait_ge(v_s, 2 * b)
                for j in range(J):
                    dst = kv_ps[:, j, :]
                    pe.matmul(dst, xnT[:, b * J + j, :], wkv_sb[:], start=True, stop=False)
                    last = pe.matmul(dst, ones_bf[:, 0:P], bias_rows[:, D:3 * D], start=False, stop=True)
                    if j % 2:
                        last.then_inc(kv_mm, 1)

            def product_nd(b):
                pe.wait_ge(q_s, b + 1)
                pe.wait_ge(kvd_s, 2 * (b + 1))
                if b >= 1:
                    pe.wait_ge(sc_s, b)
                for j in range(J):
                    last = pe.matmul(nd_ps[:, j, 0:ND], qT[:, b, j * P:(j + 1) * P],
                                     kvd[:, b, :], start=True, stop=True)
                last.then_inc(nd_mm, 1)

            def scores_T(b):
                pe.wait_ge(sc_s, b + 1)
                if b >= 2:
                    pe.wait_ge(lm_s, b - 1)
                for j in range(J):
                    last = pe.transpose(scT_ps[:, j * P:(j + 1) * P], sc[:, b * J + j, :], ident[:])
                last.then_inc(scT_mm, 1)

            def rows_T(b):
                pe.wait_ge(kvd_s, 2 * min(b + 2, B))
                for j in range(J):
                    pe.wait_ge(h_s, b * J + j + 1)
                    last = pe.transpose(hT_ps[:, j * P:(j + 1) * P], rows[:, b * J + j, 0:D], ident[:])
                last.then_inc(hT_mm, 1)

            def product_o(b):
                pe.wait_ge(scT_s, b + 1)
                pe.wait_ge(q_s, min(b + 2, B))
                if b == 0:
                    pe.wait_ge(wo_in, 16)
                for j in range(J):
                    dst = att_ps[:, j * D:(j + 1) * D]
                    pe.matmul(dst, scT[:, b * J + j, :], wo_sb[:], start=True, stop=False)
                    last = pe.matmul(dst, ones_bf[:, 0:P], bias_rows[:, 3 * D:4 * D], start=False, stop=True)
                last.then_inc(att_mm, 1)

            def logits(b):
                pe.wait_ge(hT_s, b + 1)
                pe.wait_ge(scT_s, min(b + 2, B))
                if b == B - 1:
                    pe.wait_ge(lm_s, b)
                if b == 0:
                    pe.wait_ge(wr_in, 16)
                for j in range(J):
                    last = pe.matmul(lg_ps[:, j * E:(j + 1) * E], hT[:, b * J + j, :], wr_sb[:], start=True, stop=True)
                last.then_inc(lg_mm, 1)

            def rank_sums(b):
                if b == 0:
                    pe.wait_ge(pool_const, 4)
                pe.wait_ge(onehot_s, b + 1)
                pe.wait_ge(xnT_s, B)
                if b >= 1:
                    pe.wait_ge(rkm_s, b)
                pe.wait_ge(total_s, b + 1)
                t0 = b * J
                rk = rk_ps
                pe.matmul(rk, before[:], onehot[:, tiles(b), :].rearrange("p j e -> p (j e)"), start=True, stop=False)
                for a in range(b):
                    pe.matmul(rk.rearrange("p (j e) -> p j e", e=E), ones16[:],
                              total[:, a:a + 1, :].broadcast_to([P, J, E]), start=False, stop=False)
                for j in range(J - 1):
                    last = pe.matmul(rk[:, (j + 1) * E:].rearrange("p (j e) -> p j e", e=E), ones16[:],
                                     onehot[:, t0 + j:t0 + j + 1, :].broadcast_to([P, J - 1 - j, E]), start=False,
                                     stop=j == J - 2)
                if b < B - 1:
                    last.then_inc(rk_mm, 1)
                    return
                for a in range(B):
                    last = pe.matmul(cnt_ps[:, CNT:CNT + E], ones16[:], total[:, a, :], start=a == 0, stop=a == B - 1)
                last.then_inc(cnt_mm, 1)

            def keep_warm(n):
                for _ in range(n):
                    pe.matmul(warm_ps[:], ones_bf[:, 0:P], ones_bf[:], start=True, stop=True)

            pe.wait_ge(dve_const, 1)
            keep_warm(WARM_START)
            for s in range(B + 2):
                if s < B:
                    normalised_T(s)
                if s == 0:
                    keep_warm(WARM_FIRST)
                if 1 <= s <= B:
                    product_ks(s - 1)
                if s < B:
                    product_q(s)
                if s == B:
                    keep_warm(WARM_LAST[0])
                if 1 <= s <= B:
                    product_nd(s - 1)
                if s < B:
                    product_kv(s)
                if 3 <= s <= B:
                    rank_sums(s - 3)
                if s == B:
                    keep_warm(WARM_LAST[1])
                if 1 <= s <= B:
                    scores_T(s - 1)
                if s >= 2:
                    rows_T(s - 2)
                if 1 <= s <= B:
                    product_o(s - 1)
                if s == B + 1:
                    keep_warm(WARM_LAST[4])
                if s >= 2:
                    logits(s - 2)
                if s == B:
                    keep_warm(WARM_LAST[2])
                    rank_sums(B - 2)
                    keep_warm(WARM_LAST[3])
            pe.wait_ge(b1_in, 16)
            pe.wait_ge(sc_s, B)
            pe.transpose(b1_ps[:, 0:E * FC], b1_rows[:], ident[0:E * FC, 0:E * FC]).then_inc(b1_mm, 1)
            keep_warm(WARM_LAST[5])
            rank_sums(B - 1)
            keep_warm(WARM_ROUTING)

            def slots_T(i, r, k, turn):
                if not (isinstance(i, int) and i < 2):
                    pe.wait_ge(tT_s, i - 1)
                pe.wait_ge(slot_h_in[r], turn * 16)
                pe.transpose(tT_ps[k][:, 0:P], slot_h[:, r, :], ident[:]).then_inc(tT_mm, 1)

            def hidden(i, r, k):
                pe.wait_ge(tT_s, i + 1)
                pe.wait_ge(w1_s, i + 1)
                if not (isinstance(i, int) and i < 2):
                    pe.wait_ge(hid_s, (i - 1) * FC)
                for c in range(FC):
                    last = pe.matmul(hid_ps[k][:, c * P:(c + 1) * P], w1_st[:, k, c * P:(c + 1) * P], tT[:, r, :],
                                     start=True, stop=True)
                last.then_inc(hid_mm, 1)

            def down(i, k):
                pe.wait_ge(hid_s, (i + 1) * FC)
                pe.wait_ge(w2_s, i + 1)
                if not (isinstance(i, int) and i < 2):
                    pe.wait_ge(yb_s, i - 1)
                for c in range(FC):
                    last = pe.matmul(y_ps[k][:, 0:D], hid[:, k, c, :], w2_st[:, k, c, :], start=c == 0, stop=c == FC - 1)
                last.then_inc(y_mm, 1)

            pe.wait_ge(b1_s, 1)
            slots_T(0, 0, 0, 1)
            slots_T(1, 1, 1, 1)
            hidden(0, 0, 0)
            for i in range(2):
                slots_T(i + 2, i + 2, i % 2, 1)
                hidden(i + 1, i + 1, (i + 1) % 2)
                down(i, i % 2)
            loops = (SLOT_TILES - 4) // RING
            with pe.Fori(0, loops) as m:
                for r in range(RING):
                    i = m * RING + r + 2
                    slots_T(i + 2, r, r % 2, m + 2)
                    hidden(i + 1, (r + 3) % RING, (r + 1) % 2)
                    down(i, r % 2)
            for i in range(loops * RING + 2, SLOT_TILES):
                if i + 2 < SLOT_TILES:
                    slots_T(i + 2, (i + 2) % RING, i % 2, (i + 2) // RING + 1)
                if i + 1 < SLOT_TILES:
                    hidden(i + 1, (i + 1) % RING, (i + 1) % 2)
                down(i, i % 2)


_INS = ['L0_attn_x', 'L0_attn_wq', 'L0_attn_bq', 'L0_attn_wk', 'L0_attn_bk', 'L0_attn_wv', 'L0_attn_bv', 'L0_attn_wo',
        'L0_attn_bo', 'L0_ffn_Wr', 'L0_ffn_W1', 'L0_ffn_b1', 'L0_ffn_W2', 'L0_ffn_b2']


def kernel(**inputs):
    import numpy as _np
    import concourse.bacc as _bacc
    from concourse import mybir as _mybir
    from concourse.bass_utils import run_bass_kernel_spmd as _run

    nc = _bacc.Bacc("TRN2", target_bir_lowering=False, num_devices=1)
    arrays, args = {}, []
    for name in _INS:
        a = _np.ascontiguousarray(inputs[name])
        arrays[f"in_{name}_dram"] = a
        args.append(nc.dram_tensor(f"in_{name}_dram", a.shape, _mybir.dt.from_np(a.dtype), kind="ExternalInput").ap())
    shape = inputs['L0_attn_x'].shape
    args.append(nc.dram_tensor("out_0_dram", shape, _mybir.dt.float32, kind="ExternalOutput").ap())
    preln_linear_attention_moe(nc, *args)
    r = _run(nc, [arrays], core_ids=[0])
    return r.results[0]["out_0_dram"]
```
